# Optimizing a Trainium2 kernel written in Bass

```python
import numpy as np
import jax
import jax.numpy as jnp

def _softmax(x, axis=-1):
    return jax.nn.softmax(x, axis=axis)

def _gelu(x):
    return jax.nn.gelu(x, approximate=True)

def _silu(x):
    return jax.nn.silu(x)

def _sigmoid(x):
    return jax.nn.sigmoid(x)

def _layernorm(x, axis=-1, eps=1e-05):
    m = jnp.mean(x, axis=axis, keepdims=True)
    v = jnp.var(x, axis=axis, keepdims=True)
    return (x - m) / jnp.sqrt(v + eps)

def _scatter_add(tgt, idx, src, axis=0):
    return tgt.at[idx].add(src)

def _segment_sum(src, seg, n):
    return jax.ops.segment_sum(src, seg, n)
kernel_name = 'mk_perceiver_d2_seqx_r4_1e10bf'

def setup_inputs(seed: int=0):
    np.random.seed(seed)
    _w = jnp.asarray

    def _rec_inputs():
        import jax
        import jax.numpy as jnp
        _rk = jax.random.key(seed)
        x = -0.0002928 + 1 * jax.random.normal(jax.random.fold_in(_rk, 1), (8, 64, 256), jnp.float32)
        _lenS = 64 - jax.random.randint(jax.random.fold_in(_rk, 7), (8,), 0, max(1, 64 // 4) + 1, jnp.int32)
        _lenS2 = 1601 - jax.random.randint(jax.random.fold_in(_rk, 8), (8,), 0, max(1, 1601 // 4) + 1, jnp.int32)
        _ctx_1024P = jax.random.normal(jax.random.fold_in(_rk, 11), (8, 16, 256), jnp.float32)
        _ctx_1024c = jax.random.dirichlet(jax.random.fold_in(_rk, 511), 0.3 * jnp.ones((16,), jnp.float32), (8, 1601))
        _ctx_1024t = jnp.einsum('bsk,bkd->bsd', _ctx_1024c, _ctx_1024P)
        _ctx_1024t = _ctx_1024t * jax.lax.rsqrt(jnp.mean(jnp.square(_ctx_1024t)) + 1e-12) * 0.953939
        ctx_1024 = -1.39393e-06 + 0.999914 * (_ctx_1024t + 0.3 * jax.random.normal(jax.random.fold_in(_rk, 611), (8, 1601, 256), jnp.float32))
        return (x, ctx_1024)
    x, ctx_1024 = _rec_inputs()

    def _L0_xattn_setup():
        import jax, jax.numpy as jnp
        import numpy as np
        D_MODEL = 256
        NUM_HEADS = 16
        HEAD_DIM = D_MODEL // NUM_HEADS
        BATCH = 2
        SEQ = 512

        def _split_heads(x):
            b, s, d = x.shape
            return x.reshape(b, s, NUM_HEADS, HEAD_DIM).transpose(0, 2, 1, 3)
        key = jax.random.key(seed)
        ks = jax.random.split(key, 7)
        s = 1.0 / np.sqrt(D_MODEL)
        return {'q': jax.random.normal(ks[0], (BATCH, SEQ, D_MODEL), jnp.float32), 'k': jax.random.normal(ks[1], (BATCH, SEQ, D_MODEL), jnp.float32), 'v': jax.random.normal(ks[2], (BATCH, SEQ, D_MODEL), jnp.float32), 'Wq': jax.random.normal(ks[3], (D_MODEL, D_MODEL), jnp.float32) * s, 'Wk': jax.random.normal(ks[4], (D_MODEL, D_MODEL), jnp.float32) * s, 'Wv': jax.random.normal(ks[5], (D_MODEL, D_MODEL), jnp.float32) * s, 'Wo': jax.random.normal(ks[6], (D_MODEL, D_MODEL), jnp.float32) * s}
    _L0_xattn_all = _L0_xattn_setup()
    _L0_xattn_in = {k: v for k, v in _L0_xattn_all.items() if k in ('Wq', 'Wk', 'Wv', 'Wo')}
    del _L0_xattn_all

    def _L0_attn_setup():
        import jax, jax.numpy as jnp
        import numpy as np
        HID = 256
        HEADS = 16
        HEAD_DIM = HID // HEADS
        key = jax.random.key(seed)
        ks = jax.random.split(key, 6)
        N, S = (4, 1024)
        scale = 1.0 / np.sqrt(HID)
        return {'x': jax.random.normal(ks[0], (N, S, HID), dtype=jnp.float32), 'Wq': jax.random.normal(ks[1], (HID, HID), dtype=jnp.float32) * scale, 'Wk': jax.random.normal(ks[2], (HID, HID), dtype=jnp.float32) * scale, 'Wv': jax.random.normal(ks[3], (HID, HID), dtype=jnp.float32) * scale, 'Wo': jax.random.normal(ks[4], (HID, HID), dtype=jnp.float32) * scale, 'bo': jnp.zeros((HID,), dtype=jnp.float32)}
    _L0_attn_all = _L0_attn_setup()
    _L0_attn_in = {k: v for k, v in _L0_attn_all.items() if k in ('Wq', 'Wk', 'Wv', 'Wo', 'bo')}
    del _L0_attn_all

    def _L0_ffn_setup():
        import jax, jax.numpy as jnp
        import numpy as np
        B, S, D, E = (4, 1024, 256, 8)
        key = jax.random.key(seed)
        k1, k2, k3, k4, k5 = jax.random.split(key, 5)
        scale = 1.0 / np.sqrt(D)
        return {'x': jax.random.normal(k1, (B, S, D), dtype=jnp.float32), 'Wg': jax.random.normal(k2, (D, D), dtype=jnp.float32) * scale, 'bg': jnp.zeros((D,), dtype=jnp.float32), 'We': jax.random.normal(k3, (E, D, D), dtype=jnp.float32) * scale, 'be': jnp.zeros((E, D), dtype=jnp.float32)}
    _L0_ffn_all = _L0_ffn_setup()
    _L0_ffn_in = {k: v for k, v in _L0_ffn_all.items() if k in ('Wg', 'bg', 'We', 'be')}
    del _L0_ffn_all

    def _L1_xattn_setup():
        import jax, jax.numpy as jnp
        import numpy as np
        D_MODEL = 256
        NUM_HEADS = 16
        D_K = D_MODEL // NUM_HEADS

        def _split_heads(x):
            B, S, _ = x.shape
            return x.reshape(B, S, NUM_HEADS, D_K).transpose(0, 2, 1, 3)
        key = jax.random.key(seed)
        ks = jax.random.split(key, 11)
        B, S = (2, 512)
        s = 1.0 / np.sqrt(D_MODEL)
        return {'Q': jax.random.normal(ks[0], (B, S, D_MODEL), jnp.float32), 'K': jax.random.normal(ks[1], (B, S, D_MODEL), jnp.float32), 'V': jax.random.normal(ks[2], (B, S, D_MODEL), jnp.float32), 'Wq': jax.random.normal(ks[3], (D_MODEL, D_MODEL), jnp.float32) * s, 'bq': jax.random.normal(ks[4], (D_MODEL,), jnp.float32) * s, 'Wk': jax.random.normal(ks[5], (D_MODEL, D_MODEL), jnp.float32) * s, 'bk': jax.random.normal(ks[6], (D_MODEL,), jnp.float32) * s, 'Wv': jax.random.normal(ks[7], (D_MODEL, D_MODEL), jnp.float32) * s, 'bv': jax.random.normal(ks[8], (D_MODEL,), jnp.float32) * s, 'Wo': jax.random.normal(ks[9], (D_MODEL, D_MODEL), jnp.float32) * s, 'bo': jax.random.normal(ks[10], (D_MODEL,), jnp.float32) * s}
    _L1_xattn_all = _L1_xattn_setup()
    _L1_xattn_in = {k: v for k, v in _L1_xattn_all.items() if k in ('Wq', 'bq', 'Wk', 'bk', 'Wv', 'bv', 'Wo', 'bo')}
    del _L1_xattn_all

    def _L1_attn_setup():
        import jax, jax.numpy as jnp
        import numpy as np
        LN_EPS = 1e-05
        CLAMP = 1000000.0
        key = jax.random.key(seed)
        k0, k1, k2, k3 = jax.random.split(key, 4)
        Bsz, L, D, N = (8, 512, 256, 64)
        x = jax.random.normal(k0, (Bsz, L, D), dtype=jnp.float32)
        A = jax.random.normal(k1, (N, N), dtype=jnp.float32) * 0.01
        B = jax.random.normal(k2, (N, D), dtype=jnp.float32) * 0.01
        C = jax.random.normal(k3, (D, N), dtype=jnp.float32) * 0.01
        gamma = jnp.ones((D,), dtype=jnp.float32)
        beta = jnp.zeros((D,), dtype=jnp.float32)
        return {'x': x, 'A': A, 'B': B, 'C': C, 'gamma': gamma, 'beta': beta}
    _L1_attn_all = _L1_attn_setup()
    _L1_attn_in = {k: v for k, v in _L1_attn_all.items() if k in ('A', 'B', 'C', 'gamma', 'beta')}
    del _L1_attn_all

    def _L1_ffn_setup():
        import jax, jax.numpy as jnp
        import numpy as np
        H = 256
        I = 1024
        E = 8
        K = 2
        B, S = (2, 512)

        def _moe_linear(x, router_w, expert_w):
            n_exp = router_w.shape[0]
            logits = x @ router_w.T
            vals, idx = jax.lax.top_k(logits, K)
            probs = jax.nn.softmax(vals, axis=-1)
            onehot = jax.nn.one_hot(idx, n_exp, dtype=x.dtype)
            combine = jnp.einsum('tk,tke->te', probs, onehot)
            out = jnp.zeros((x.shape[0], expert_w.shape[1]), x.dtype)
            for e in range(n_exp):
                out = out + combine[:, e:e + 1] * (x @ expert_w[e].T)
            return out
        key = jax.random.key(seed)
        ks = jax.random.split(key, 7)
        init = lambda k, shape, fan_in: jax.random.normal(k, shape, jnp.float32) / np.float32(np.sqrt(fan_in))
        return {'x': jax.random.normal(ks[0], (B, S, H), jnp.float32), 'router_gate': init(ks[1], (E, H), H), 'w_gate': init(ks[2], (E, I, H), H), 'router_up': init(ks[3], (E, H), H), 'w_up': init(ks[4], (E, I, H), H), 'router_down': init(ks[5], (E, I), I), 'w_down': init(ks[6], (E, H, I), I)}
    _L1_ffn_all = _L1_ffn_setup()
    _L1_ffn_in = {k: v for k, v in _L1_ffn_all.items() if k in ('router_gate', 'w_gate', 'router_up', 'w_up', 'router_down', 'w_down')}
    del _L1_ffn_all
    return {'x': x, 'ctx_1024': ctx_1024, 'L0_xattn_Wq': _L0_xattn_in['Wq'], 'L0_xattn_Wk': _L0_xattn_in['Wk'], 'L0_xattn_Wv': _L0_xattn_in['Wv'], 'L0_xattn_Wo': _L0_xattn_in['Wo'], 'L0_attn_Wq': _L0_attn_in['Wq'], 'L0_attn_Wk': _L0_attn_in['Wk'], 'L0_attn_Wv': _L0_attn_in['Wv'], 'L0_attn_Wo': _L0_attn_in['Wo'], 'L0_attn_bo': _L0_attn_in['bo'], 'L0_ffn_Wg': _L0_ffn_in['Wg'], 'L0_ffn_bg': _L0_ffn_in['bg'], 'L0_ffn_We': _L0_ffn_in['We'], 'L0_ffn_be': _L0_ffn_in['be'], 'L1_xattn_Wq': _L1_xattn_in['Wq'], 'L1_xattn_bq': _L1_xattn_in['bq'], 'L1_xattn_Wk': _L1_xattn_in['Wk'], 'L1_xattn_bk': _L1_xattn_in['bk'], 'L1_xattn_Wv': _L1_xattn_in['Wv'], 'L1_xattn_bv': _L1_xattn_in['bv'], 'L1_xattn_Wo': _L1_xattn_in['Wo'], 'L1_xattn_bo': _L1_xattn_in['bo'], 'L1_attn_A': _L1_attn_in['A'], 'L1_attn_B': _L1_attn_in['B'], 'L1_attn_C': _L1_attn_in['C'], 'L1_attn_gamma': _L1_attn_in['gamma'], 'L1_attn_beta': _L1_attn_in['beta'], 'L1_ffn_router_gate': _L1_ffn_in['router_gate'], 'L1_ffn_w_gate': _L1_ffn_in['w_gate'], 'L1_ffn_router_up': _L1_ffn_in['router_up'], 'L1_ffn_w_up': _L1_ffn_in['w_up'], 'L1_ffn_router_down': _L1_ffn_in['router_down'], 'L1_ffn_w_down': _L1_ffn_in['w_down']}

def reference(x, ctx_1024, L0_xattn_Wq, L0_xattn_Wk, L0_xattn_Wv, L0_xattn_Wo, L0_attn_Wq, L0_attn_Wk, L0_attn_Wv, L0_attn_Wo, L0_attn_bo, L0_ffn_Wg, L0_ffn_bg, L0_ffn_We, L0_ffn_be, L1_xattn_Wq, L1_xattn_bq, L1_xattn_Wk, L1_xattn_bk, L1_xattn_Wv, L1_xattn_bv, L1_xattn_Wo, L1_xattn_bo, L1_attn_A, L1_attn_B, L1_attn_C, L1_attn_gamma, L1_attn_beta, L1_ffn_router_gate, L1_ffn_w_gate, L1_ffn_router_up, L1_ffn_w_up, L1_ffn_router_down, L1_ffn_w_down):
    import jax
    import jax.numpy as jnp

    def _L0_xattn_ref(q, k, v, Wq, Wk, Wv, Wo):
        import jax, jax.numpy as jnp
        import numpy as np
        D_MODEL = 256
        NUM_HEADS = 16
        HEAD_DIM = D_MODEL // NUM_HEADS
        BATCH = 2
        SEQ = 512

        def _split_heads(x):
            b, s, d = x.shape
            return x.reshape(b, s, NUM_HEADS, HEAD_DIM).transpose(0, 2, 1, 3)
        qh = _split_heads(q @ Wq.T)
        kh = _split_heads(k @ Wk.T)
        vh = _split_heads(v @ Wv.T)
        scale = 1.0 / jnp.sqrt(jnp.asarray(HEAD_DIM, qh.dtype))
        scores = jnp.einsum('bhqd,bhkd->bhqk', qh, kh) * scale
        attn = jax.nn.softmax(scores, axis=-1)
        out = jnp.einsum('bhqk,bhkd->bhqd', attn, vh)
        out = out.transpose(0, 2, 1, 3).reshape(q.shape[0], q.shape[1], D_MODEL)
        return out @ Wo.T

    def _L0_attn_ref(x, Wq, Wk, Wv, Wo, bo):
        import jax, jax.numpy as jnp
        import numpy as np
        HID = 256
        HEADS = 16
        HEAD_DIM = HID // HEADS
        N, S, _ = x.shape
        q = (x @ Wq).reshape(N, S, HEADS, HEAD_DIM)
        k = (x @ Wk).reshape(N, S, HEADS, HEAD_DIM)
        v = (x @ Wv).reshape(N, S, HEADS, HEAD_DIM)
        q = jnp.swapaxes(q, 1, 2)
        k = jnp.swapaxes(k, 1, 2)
        v = jnp.swapaxes(v, 1, 2)
        energy = jnp.einsum('nahd,nbhd->nab', q, k)
        attention = jax.nn.softmax(energy / np.sqrt(HEAD_DIM), axis=2)
        out = jnp.einsum('nab,nbsd->nasd', attention, v)
        out = out.reshape(N, S, HID)
        return out @ Wo + bo

    def _L0_ffn_ref(x, Wg, bg, We, be):
        import jax, jax.numpy as jnp
        import numpy as np
        B, S, D, E = (4, 1024, 256, 8)
        probs = jax.nn.softmax(x @ Wg + bg, axis=-1)
        idx = jnp.argmax(probs, axis=-1)
        p = jnp.take_along_axis(probs, idx[..., None], axis=-1)[..., 0]
        e_idx = idx % We.shape[0]
        h = jax.nn.relu(jnp.einsum('bsd,edf->besf', x, We) + be[None, :, None, :])
        onehot = jax.nn.one_hot(e_idx, We.shape[0], dtype=x.dtype)
        out = jnp.einsum('besf,bse->bsf', h, onehot) * p[..., None]
        return out

    def _L1_xattn_ref(Q, K, V, Wq, bq, Wk, bk, Wv, bv, Wo, bo):
        import jax, jax.numpy as jnp
        import numpy as np
        D_MODEL = 256
        NUM_HEADS = 16
        D_K = D_MODEL // NUM_HEADS

        def _split_heads(x):
            B, S, _ = x.shape
            return x.reshape(B, S, NUM_HEADS, D_K).transpose(0, 2, 1, 3)
        q = _split_heads(Q @ Wq.T + bq)
        k = _split_heads(K @ Wk.T + bk)
        v = _split_heads(V @ Wv.T + bv)
        scale = 1.0 / jnp.sqrt(jnp.asarray(D_K, q.dtype))
        scores = jnp.einsum('bhqd,bhkd->bhqk', q, k) * scale
        attn = jax.nn.softmax(scores, axis=-1)
        out = jnp.einsum('bhqk,bhkd->bhqd', attn, v)
        B, H, S, dk = out.shape
        out = out.transpose(0, 2, 1, 3).reshape(B, S, H * dk)
        return out @ Wo.T + bo

    def _L1_attn_ref(x, A, B, C, gamma, beta):
        import jax, jax.numpy as jnp
        import numpy as np
        LN_EPS = 1e-05
        CLAMP = 1000000.0
        Bsz = x.shape[0]
        N = A.shape[0]
        uB = jnp.einsum('bld,nd->lbn', x, B)

        def step(state, u_t):
            s = state @ A.T + u_t
            return (s, s)
        init = jnp.zeros((Bsz, N), dtype=x.dtype)
        _, states = jax.lax.scan(step, init, uB)
        y = jnp.einsum('lbn,dn->bld', states, C)
        act = jax.nn.gelu(y, approximate=False)
        mean = jnp.mean(act, axis=-1, keepdims=True)
        var = jnp.var(act, axis=-1, keepdims=True)
        norm = (act - mean) / jnp.sqrt(var + LN_EPS) * gamma + beta
        return jnp.nan_to_num(norm, nan=0.0, posinf=CLAMP, neginf=-CLAMP)

    def _L1_ffn_ref(x, router_gate, w_gate, router_up, w_up, router_down, w_down):
        import jax, jax.numpy as jnp
        import numpy as np
        H = 256
        I = 1024
        E = 8
        K = 2
        B, S = (2, 512)

        def _moe_linear(x, router_w, expert_w):
            n_exp = router_w.shape[0]
            logits = x @ router_w.T
            vals, idx = jax.lax.top_k(logits, K)
            probs = jax.nn.softmax(vals, axis=-1)
            onehot = jax.nn.one_hot(idx, n_exp, dtype=x.dtype)
            combine = jnp.einsum('tk,tke->te', probs, onehot)
            out = jnp.zeros((x.shape[0], expert_w.shape[1]), x.dtype)
            for e in range(n_exp):
                out = out + combine[:, e:e + 1] * (x @ expert_w[e].T)
            return out
        b, s, h = x.shape
        xt = x.reshape(b * s, h)
        g = _moe_linear(xt, router_gate, w_gate)
        u = _moe_linear(xt, router_up, w_up)
        inter = jax.nn.silu(g) * u
        d = _moe_linear(inter, router_down, w_down)
        return d.reshape(b, s, h)
    x = x + _L0_xattn_ref(_layernorm(x, axis=-1), ctx_1024, ctx_1024, L0_xattn_Wq, L0_xattn_Wk, L0_xattn_Wv, L0_xattn_Wo)
    x = x + _L0_attn_ref(_layernorm(x, axis=-1), L0_attn_Wq, L0_attn_Wk, L0_attn_Wv, L0_attn_Wo, L0_attn_bo)
    x = x + _L0_ffn_ref(_layernorm(x, axis=-1), L0_ffn_Wg, L0_ffn_bg, L0_ffn_We, L0_ffn_be)
    x = x + _L1_xattn_ref(_layernorm(x, axis=-1), ctx_1024, ctx_1024, L1_xattn_Wq, L1_xattn_bq, L1_xattn_Wk, L1_xattn_bk, L1_xattn_Wv, L1_xattn_bv, L1_xattn_Wo, L1_xattn_bo)
    x = x + _L1_attn_ref(_layernorm(x, axis=-1), L1_attn_A, L1_attn_B, L1_attn_C, L1_attn_gamma, L1_attn_beta)
    x = x + _L1_ffn_ref(_layernorm(x, axis=-1), L1_ffn_router_gate, L1_ffn_w_gate, L1_ffn_router_up, L1_ffn_w_up, L1_ffn_router_down, L1_ffn_w_down)
    return x

_drawn_inputs = setup_inputs


def setup_inputs(seed=0):
    import zlib

    import numpy as np

    out = dict(_drawn_inputs(seed))
    spreads = {'L0_attn_bo': (0.0, 0.1),
     'L0_ffn_bg': (0.0, 0.464),
     'L0_ffn_be': (0.0, 0.697),
     'L1_attn_gamma': (1.0, 0.2),
     'L1_attn_beta': (0.0, 0.1)}
    factors = {'L1_xattn_bk': 8.0}
    for name, (base, spread) in spreads.items():
        noise = np.random.default_rng([zlib.crc32(name.encode()), seed]).standard_normal(out[name].shape)
        drawn = base * np.exp(spread * noise) if base else spread * noise
        out[name] = jnp.asarray(drawn.astype(out[name].dtype))
    for name, factor in factors.items():
        out[name] = (out[name] * factor).astype(out[name].dtype)
    return out
```

```python
from contextlib import ExitStack

import concourse.bass as bass
import numpy as np
from concourse import mybir

F32 = mybir.dt.float32
F16 = mybir.dt.float16
U32 = mybir.dt.uint32
ALU = mybir.AluOpType
ACT = mybir.ActivationFunctionType
AX = mybir.AxisListType

P = 128
D = 256
KC = D // P
B = 8
NQ = 64
T = B * NQ
TT = T // P
H = 16
DH = D // H
NP = H // 2
S = 1601
KT = -(-S // P)
HALF = (S + 1) // 2
E = 8
FI = 1024
IT = FI // P
N = 64
BANK = 512
STACK = 96
VW = 65
W_SCALE = 256.0
M_SCALE = 64.0
LN_EPS = 1e-5
F32_MAX = 3.4028234663852886e38
CLAMP = 1e6

HALVES = [(0, HALF), (HALF, S - HALF)]
TILE_ROWS = [min(P, S - P * k) for k in range(KT)]
V_TILES = [range(4 * v, min(4 * v + 4, KT)) for v in range(4)]
PRING = 4

PROLOGUE_UNITS = ["K0", "K1", "K2", "K3", "V0", "V1", "V2", "V3"] + [f"P{i}" for i in range(16)] + ["T"]
STEP_UNITS = {0: ["K0"], 1: ["K1"], 2: ["K2"], 3: ["K3"], 5: ["P0", "P1"], 6: ["P2", "P3"],
              7: ["V0", "P4"], 8: ["P5", "P6"], 9: ["P7", "P8"], 10: ["P9", "P10"],
              11: ["V1", "P11", "P12", "P13"], 12: ["P14", "P15"]}
BODY_UNITS = [n for k in range(KT) for n in STEP_UNITS.get(k, [])] + ["T", "V2", "V3", "O"]
PER_LAYER = len(PROLOGUE_UNITS) + len(BODY_UNITS) * (B - 1) + 1
assert len(BODY_UNITS) == 26 and PER_LAYER % 2 == 0 and len(PROLOGUE_UNITS) == 25


def ring_back(u, k):
    uses = [kk + 1 - u for kk in range(KT)] + [kk + u for kk in range(k)]
    for back in range(1, len(uses) + 1):
        if uses[-back] % PRING == (k + u) % PRING:
            return back
    raise AssertionError


def build(nc, d, out):
    with ExitStack() as ctx:
        def sb(stack, name, shape, dt=F32):
            return stack.enter_context(nc.sbuf_tensor(name, shape, dt))

        sems = {}

        def sem(name):
            if name not in sems:
                sems[name] = ctx.enter_context(nc.semaphore(name))
            return sems[name]

        def need(eng, name, value):
            if isinstance(value, int) and value <= 0:
                return
            eng.wait_ge(sem(name), value)

        x = sb(ctx, "x", [P, TT, D])
        oT = sb(ctx, "oT", [P, 2, T])
        wkv32 = sb(ctx, "wkv32", [P, KC, 2, D])
        wkh = [sb(ctx, f"wkh{i}", [P, KC, D], F16) for i in range(2)]
        wkl = [sb(ctx, f"wkl{i}", [P, KC, D], F16) for i in range(2)]
        wvh = [sb(ctx, f"wvh{i}", [P, KC, D], F16) for i in range(2)]
        wvl = [sb(ctx, f"wvl{i}", [P, KC, D], F16) for i in range(2)]
        wq = sb(ctx, "wq", [P, KC, D])
        wo = sb(ctx, "wo", [P, 2, D])
        aw = sb(ctx, "aw", [P, 4, KC, D])
        ident = sb(ctx, "ident", [P, P])
        ident16 = sb(ctx, "ident16", [P, P], F16)
        small = sb(ctx, "small", [P, 24])
        bias = sb(ctx, "bias", [P, 3, 2])
        rows = sb(ctx, "rows", [P, 5, D])
        am = sb(ctx, "am", [N, 6, 2, N])
        half = sb(ctx, "half", [P, TT])
        SM_EVEN, SM_IOTA, SM_MIX = 0, 2, 10

        lnb = {}

        def ln_buffers(stack, tag):
            lnb[tag] = dict(
                xn=sb(stack, f"xn_{tag}", [P, TT, D]), xnT=sb(stack, f"xnT_{tag}", [P, KC, T]),
                h=sb(stack, f"xh_{tag}", [P, KC, T], F16), l=sb(stack, f"xl_{tag}", [P, KC, T], F16),
                st=sb(stack, f"st_{tag}", [P, TT, 6]), mv=sb(stack, f"mv_{tag}", [P, TT, 2]),
                ve=sb(stack, f"ve_{tag}", [P, TT]), rstd=sb(stack, f"rs_{tag}", [P, TT]))

        with ExitStack() as s:
            ln_buffers(s, "moe")
            xch = [sb(s, f"xch{r}", [P, E, KC, T], F16) for r in range(2)]
            xcl = [sb(s, f"xcl{r}", [P, E, KC, T], F16) for r in range(2)]
            w32 = sb(s, "w32", [P, 3, KC * E * P])
            wh = sb(s, "wh", [P, 2, KC * E * P], F16)
            wl = sb(s, "wl", [P, 2, KC * E * P], F16)
            xc = sb(s, "xc", [P, 2, TT, D])
            ih = sb(s, "ih", [P, IT, T], F16)
            il = sb(s, "il", [P, IT, T], F16)
            i32 = sb(s, "i32", [P, 2, T])
            sg = sb(s, "sg", [P, 3, T])
            rw = sb(s, "rw", [P, KC, 2, E])
            rdw = sb(s, "rdw", [P, IT, E])
            ldT = sb(s, "ldT", [E, T])
            lgm = sb(s, "lgm", [P, 3 * TT, E])
            top = sb(s, "top", [P, 3 * TT, 8])
            topi = sb(s, "topi", [P, 3 * TT, 8], U32)
            topf = sb(s, "topf", [P, 3 * TT, 2])
            pr = sb(s, "pr", [P, 3 * TT, 2])
            prt = sb(s, "prt", [P, 3 * TT, 2])
            cmb = sb(s, "cmb", [P, 3 * TT, E])
            cmb2 = sb(s, "cmb2", [P, 3 * TT, E])
        c32 = sb(ctx, "c32", [P, 2, KC, HALF])
        ch = [sb(ctx, f"ch{i}", [P, KC, S], F16) for i in range(2)]
        cl = [sb(ctx, f"cl{i}", [P, KC, S], F16) for i in range(2)]
        with ExitStack() as s:
            ln_buffers(s, "mid")
            q32 = sb(s, "q32", [P, 2, T])
            qh = sb(s, "qh", [P, 2, T], F16)
            ql = sb(s, "ql", [P, 2, T], F16)
            a_q = sb(s, "a_q", [P, TT, DH, H, 4])
            a_k = sb(s, "a_k", [P, TT, D])
            a_v = sb(s, "a_v", [P, TT, D])
            a_w = sb(s, "a_w", [P, TT, D])
            a_wT = sb(s, "a_wT", [P, KC, T])
            a_z = sb(s, "a_z", [P, TT, D])
            a_e = sb(s, "a_e", [P, TT, H])
            a_p = sb(s, "a_p", [P, TT, H])
            a_mT = sb(s, "a_mT", [P, TT, P])
            a_m = sb(s, "a_m", [P, TT, P])
            a_s = sb(s, "a_s", [P, 4, TT])
            fw32 = sb(s, "fw32", [P, KC, E * D])
            fwh = sb(s, "fwh", [P, KC, E * D], F16)
            fwl = sb(s, "fwl", [P, KC, E * D], F16)
            fb32 = sb(s, "fb32", [1, E * D])
            fbh = sb(s, "fbh", [1, E * D], F16)
            fbl = sb(s, "fbl", [1, E * D], F16)
            ones16 = sb(s, "ones16", [1, P], F16)
            wg = sb(s, "wg", [P, KC, D])
            lg = sb(s, "lg", [P, TT, D])
            ex = sb(s, "ex", [P, TT, D])
            f_s = sb(s, "f_s", [P, 3, TT])
            f_t = sb(s, "f_t", [P, TT, 8])
            f_i = sb(s, "f_i", [P, TT, 8], U32)
            f_m = sb(s, "f_m", [P, TT, 1], U32)
            f_f = sb(s, "f_f", [P, TT])
            f_w = sb(s, "f_w", [P, TT, E])
            f_y = sb(s, "f_y", [P, 4, D])
        with ExitStack() as s:
            ln_buffers(s, "ssm")
            bT = sb(s, "bT", [P, KC, N])
            cT = sb(s, "cT", [N, D])
            st_s = sb(s, "st_s", [N, B, NQ])
            g_a = sb(s, "g_a", [P, TT, D])
            g_n = sb(s, "g_n", [P, TT, D])
            g_m = sb(s, "g_m", [P, TT, D])
            g_z = sb(s, "g_z", [P, TT, D])
            g_f = sb(s, "g_f", [P, TT, D], U32)
        p32 = sb(ctx, "p32", [P, 2, H * NQ])
        ph = sb(ctx, "ph", [P, PRING, H * NQ], F16)
        pl = sb(ctx, "pl", [P, PRING, H * NQ], F16)
        qs = sb(ctx, "qs", [STACK, B, NP, P], F16)
        qcur = [sb(ctx, f"qcur{i}", [STACK + 1, NP, P], F16) for i in range(2)]
        ks = [sb(ctx, f"ks{i}", [STACK + 1, NP, S], F16) for i in range(2)]
        k32 = sb(ctx, "k32", [P, 2, HALF])
        kh = sb(ctx, "kh", [P, 2, S], F16)
        kl = sb(ctx, "kl", [P, 2, S], F16)
        v = sb(ctx, "v", [P, KT, NP, VW], F16)
        mpart = sb(ctx, "mpart", [P, NP, 2])
        m32 = sb(ctx, "m32", [P, NP])
        m16 = sb(ctx, "m16", [P, NP], F16)
        rinv = sb(ctx, "rinv", [P, 2, 4])
        osum = sb(ctx, "osum", [P, 2, 4, DH])
        onrm = sb(ctx, "onrm", [P, 2, 4, DH])

        ps = ctx.enter_context(nc.psum_tensor("ps", [P, 8, BANK], F32))
        flat = ps[:, :, :].rearrange("p b c -> p (b c)")
        slot = [flat[:, 2048 + 1024 * i:3072 + 1024 * i] for i in range(2)]
        pvb = ps[:, 2:4, 0:4 * VW].rearrange("p b (j c) -> p b j c", c=VW)

        block = ctx.enter_context(nc.Block())

        def unit(layer, b, name, prologue=False, last=False):
            if prologue:
                j, base = PROLOGUE_UNITS.index(name), 0
            else:
                j = 0 if last else BODY_UNITS.index(name)
                base = len(PROLOGUE_UNITS)
            return (base + j) % 2, (PER_LAYER // 2) * layer + 13 * b + (base + j) // 2

        def heads_by_dim(q):
            return q.rearrange("p (a c) -> p c a", a=H).unsqueeze(3).broadcast_to([P, DH, H, 4])

        def each_batch(eng, layer, body):
            body(0, 0)
            with eng.Fori(0, (B - 2) // 2) as i:
                body(2 * i + 1, 1)
                body(2 * i + 2, 0)
            body(B - 1, 1)

        @block.sync
        def _(sp):
            def load(dst, src, name):
                sp.dma_start(dst, src).then_inc(sem(name), 16)

            def load_ctx(g, b):
                for h, (k0, w) in enumerate(HALVES):
                    need(sp, "clo_done", 2 * g + h - 1)
                    load(c32[:, h, :, 0:w], d["ctxT"][b, :, :, k0:k0 + w], f"ctx_in{h}")

            def restack(g, u):
                need(sp, "main_mm", 26 * (g - 1))
                for mt in range(2):
                    sp.wait_ge(sem("klo_done"), 4 * g + 2 * mt + 2)
                    for j in range(4):
                        r, pair = slice(32 * j, 32 * j + 32), 4 * mt + j
                        load(ks[u][0:32, pair, :], kh[r, mt, :], f"stacked{mt}")
                        load(ks[u][32:64, pair, :], kl[r, mt, :], f"stacked{mt}")
                        load(ks[u][64:96, pair, :], kh[r, mt, :], f"stacked{mt}")

            load(x[:, :, :], d["x"], "x_in")
            for layer in range(2):
                if layer == 0:
                    load(wkv32[:, :, :, :], d["wkv"][0], "wkv0_in")
                    load_ctx(0, 0)
                    load_ctx(1, 1)
                else:
                    sp.wait_ge(sem("mid_done"), 3)
                g0 = B * layer
                for u in range(2):
                    load(ks[u][STACK:STACK + 1, :, :], d["ones"], "ones_in")
                restack(g0, 0)
                if layer == 0:
                    load_ctx(2, 2)

                def body(b, u):
                    g = g0 + b
                    lastb = isinstance(b, int) and b == B - 1
                    if not lastb:
                        restack(g + 1, 1 - u)
                    if not (layer == 1 and lastb):
                        load_ctx(g + 3, (b + 3) % B)

                each_batch(sp, layer, body)

                if layer == 0:
                    sp.wait_ge(sem("a_v"), 1)
                    load(d["scratch"].rearrange("(t p) c -> p t c", p=P), a_v[:, :, :], "scratch_out")
                    sp.wait_ge(sem("scratch_out"), 16)
                    for b in range(B):
                        src = d["scratch"][NQ * b:NQ * b + NQ, :].rearrange("(q s) (h c) -> h q s c", s=H, h=H)
                        for h in range(H):
                            r = NQ * (b % 2) + 4 * h
                            load(a_w[r:r + 4, b // 2, :].rearrange("p (s c) -> p s c", s=H), src[h], "a_w_in")
            sp.wait_ge(sem("moe_free"), 3)
            for h in range(2):
                sp.wait_ge(sem(f"ctx_in{h}"), 16 * (2 * B + 2))
            load(rw[:, :, :, :], d["rw"], "rw_in")
            load(rdw[:, :, :], d["rdw"], "rw_in")
            for w in range(2 * IT):
                if w >= 3:
                    sp.wait_ge(sem("wlo_done"), w - 2)
                load(w32[:, w % 3, :], d["wgu"][w], f"w_in{w % 3}")
            for e in range(E):
                w = 2 * IT + e
                sp.wait_ge(sem("wlo_done"), w - 2)
                load(w32[:, w % 3, :], d["wd"][e], f"w_in{w % 3}")
            sp.wait_ge(sem("x_final"), 1)
            load(out, x[:, :, :], "out_done")
            sp.wait_ge(sem("out_done"), 16)

        @block.gpsimd
        def _(pool):
            def load(dst, src, name):
                pool.dma_start(dst, src).then_inc(sem(name), 16)

            powers = [0]

            def inverse_root(tag):
                powers[0] += 1
                pool.wait_ge(sem("var_ready"), powers[0])
                nc.gpsimd.tensor_tensor(lnb[tag]["rstd"][:, :], lnb[tag]["ve"][:, :], half[:, :], ALU.pow)\
                  .then_inc(sem("rstd_ready"), 1)

            nc.gpsimd.memset(half[:, :], -0.5).then_inc(sem("half_ready"), 1)
            load(ident[:, :], d["ident"], "const_in")
            load(small[:, :], d["small"], "const_in")
            load(bias[:, :, :], d["bias"], "const_in")
            load(rows[:, :, :], d["rows"], "const_in")
            load(am[:, 0, :, :], d["am"], "am_in")
            load(wq[:, :, :], d["wq"][0], "wq_in")
            load(wo[:, :, :], d["wo"][0], "wo_in")
            load(aw[:, :, :, :], d["aw"], "aw_in")

            def cross(layer):
                g0 = B * layer
                nc.gpsimd.memset(v[:, :, :, 32:33], 1.0).then_inc(sem("v_ones"), 1)

                def klo(g, units):
                    for ku in units:
                        mt, (k0, w) = ku // 2, HALVES[ku % 2]
                        pool.wait_ge(sem("khi_done"), 4 * g + ku + 1)
                        nc.gpsimd.tensor_tensor(kl[:, mt, k0:k0 + w], k32[:, ku % 2, 0:w], kh[:, mt, k0:k0 + w],
                                                ALU.subtract).then_inc(sem("klo_done"), 1)

                klo(g0, range(4))

                def body(b, u):
                    g = g0 + b
                    lastb = isinstance(b, int) and b == B - 1
                    for k in range(KT):
                        n = TILE_ROWS[k]
                        buf = (k + u) % PRING
                        pool.wait_ge(sem("phi_done"), 13 * g + k + 1)
                        nc.gpsimd.tensor_tensor(pl[0:n, buf, :], p32[0:n, (u + k) % 2, :], ph[0:n, buf, :],
                                                ALU.subtract).then_inc(sem("plo_done"), 1)
                        if not lastb and f"K{k}" in STEP_UNITS.get(k, []):
                            klo(g + 1, [k])

                each_batch(pool, layer, body)

            pool.wait_ge(sem("half_ready"), 1)
            inverse_root("mid")
            cross(0)
            pool.wait_ge(sem("x_cross"), 1)
            pool.wait_ge(sem("mid_free"), 1)
            load(fw32[:, :, :], d["fw"], "fw_in")
            load(fb32[:, :], d["fb"], "fw_in")
            load(wg[:, :, :], d["wg"], "wg_in")
            nc.gpsimd.memset(ones16[:, :], 1.0).then_inc(sem("ones16"), 1)
            load(wq[:, :, :], d["wq"][1], "wq_in")
            load(wo[:, :, :], d["wo"][1], "wo_in")
            load(wkv32[:, :, :, :], d["wkv"][1], "wkv1_in")
            for _ in range(3):
                inverse_root("mid")
            pool.wait_ge(sem("mid_done"), 3)
            cross(1)
            pool.wait_ge(sem("x_cross"), 2)
            load(bT[:, :, :], d["bT"], "ssm_in")
            load(cT[:, :], d["cT"], "ssm_in")
            inverse_root("ssm")
            inverse_root("ssm")
            inverse_root("moe")
            for it in range(IT):
                pool.wait_ge(sem("ihi_done"), it + 1)
                nc.gpsimd.tensor_tensor(il[:, it, :], i32[:, it % 2, :], ih[:, it, :],
                                        ALU.subtract).then_inc(sem("ilo_done"), 1)

        @block.tensor
        def _(pe):
            def mm(o, lhsT, rhs, start, stop, shared=False):
                return nc.tensor.matmul(o, lhsT, rhs, start=start, stop=stop, skip_group_check=shared)

            def use_slot(place):
                s, used = place
                need(pe, f"slot_freed{s}", used)
                return slot[s]

            def k_unit(layer, g, u, ku, place):
                mt, (k0, w) = ku // 2, HALVES[ku % 2]
                o = use_slot(place)
                pe.wait_ge(sem("clo_done"), 2 * g + ku % 2 + 1)
                spans = [(0, BANK), (BANK, w)]
                for kc in range(KC):
                    for n, (a, c) in enumerate(((wkh, ch), (wkh, cl), (wkl, ch))):
                        for a0, a1 in spans:
                            last = mm(o[:, a0:a1], a[layer][:, kc, mt * P:mt * P + P], c[u][:, kc, k0 + a0:k0 + a1],
                                      kc == 0 and n == 0, kc == KC - 1 and n == 2)
                last.then_inc(sem("k_mm"), 1)

            def v_unit(layer, g, u, vu, place):
                o = use_slot(place)
                pe.wait_ge(sem("clo_done"), 2 * g + (1 if vu == 0 else 2))
                for i, kt in enumerate(V_TILES[vu]):
                    n = TILE_ROWS[kt]
                    for kc in range(KC):
                        for m, (c, w) in enumerate(((ch, wvh), (ch, wvl), (cl, wvh))):
                            last = mm(o[0:n, D * i:D * i + D], c[u][:, kc, P * kt:P * kt + n], w[layer][:, kc, :],
                                      kc == 0 and m == 0, kc == KC - 1 and m == 2)
                last.then_inc(sem("v_mm"), 1)

            def p_unit(g, u, i, place):
                j, (k0, w) = i // 2, HALVES[i % 2]
                if i == 0:
                    pe.wait_ge(sem("qcur_ready"), g + 1)
                if i % 8 == 0:
                    pe.wait_ge(sem(f"stacked{i // 8}"), 16 * 12 * (g + 1))
                o = use_slot(place)
                for a0, a1 in ((0, BANK), (BANK, w)):
                    last = mm(o[:, a0:a1], qcur[u][0:STACK, j, :], ks[u][0:STACK, j, k0 + a0:k0 + a1], True, True)
                last.then_inc(sem("p_mm"), 1)

            def t_unit(g, place):
                o = use_slot(place)
                pe.wait_ge(sem("m_ready"), g + 1)
                for j in range(NP):
                    last = mm(o[0:1, P * j:P * j + P], m16[:, j:j + 1], ident16[:, :], True, True)
                last.then_inc(sem("t_mm"), 1)

            def o_unit(g, place):
                o = use_slot(place)
                pe.wait_ge(sem("o_norm"), g + 1)
                nc.tensor.transpose(o[:, 0:P], onrm[:, :, :, :].rearrange("p b j d -> p (b j d)"),
                                    ident[:, :]).then_inc(sem("o_mm"), 1)

            def run_unit(layer, g, u, name, place):
                kind, i = name[0], int(name[1:] or 0)
                if kind == "K":
                    k_unit(layer, g, u, i, place)
                elif kind == "V":
                    v_unit(layer, g, u, i, place)
                elif kind == "P":
                    p_unit(g, u, i, place)
                else:
                    t_unit(g, place)

            def scores(g, u, k):
                n = TILE_ROWS[k]
                if k == 0:
                    pe.wait_ge(sem("row_done"), g + 1)
                for hb in range(2):
                    need(pe, "exp_done", 26 * g + 2 * k - 1 + hb)
                    for jj in range(4):
                        j = 4 * hb + jj
                        last = mm(ps[0:n, hb, P * jj:P * jj + P], ks[u][:, j, P * k:P * k + n], qcur[u][:, j, :],
                                  True, True)
                    last.then_inc(sem("main_mm"), 1)

            def weigh(g, u, k):
                n, buf = TILE_ROWS[k], (k + u) % PRING
                if k == 0:
                    need(pe, "o_norm", g)
                if k % 4 == 0:
                    pe.wait_ge(sem("vlo_done"), 4 * g + k // 4 + 1)
                pe.wait_ge(sem("plo_done"), 13 * g + k + 1)
                for j in range(NP):
                    o = pvb[:, j // 4, j % 4, :]
                    mm(o[:, :], ph[0:n, buf, P * j:P * j + P], v[0:n, k, j, :], k == 0 and j % 4 == 0, k == KT - 1, True)
                    last = mm(o[:, 0:33], pl[0:n, buf, P * j:P * j + P], v[0:n, k, j, 0:33], False, k == KT - 1, True)
                last.then_inc(sem("pv_mm"), 1)

            def cross(layer):
                g0 = B * layer
                pe.wait_ge(sem("kvw_ready"), layer + 1)
                for name in PROLOGUE_UNITS:
                    if name == "P0":
                        q_projection(layer)
                    run_unit(layer, g0, 0, name, unit(layer, 0, name, prologue=True))
                pe.wait_ge(sem("ones_in"), 32 * (layer + 1))

                def body(b, u):
                    g = g0 + b
                    lastb = isinstance(b, int) and b == B - 1
                    for k in range(KT):
                        scores(g, u, k)
                        if not lastb:
                            for name in STEP_UNITS.get(k, []):
                                run_unit(layer, g + 1, 1 - u, name, unit(layer, b, name))
                        if k >= 2:
                            weigh(g, u, k - 2)
                    weigh(g, u, KT - 2)
                    if not lastb:
                        run_unit(layer, g + 1, 1 - u, "T", unit(layer, b, "T"))
                        run_unit(layer, g + 1, 1 - u, "V2", unit(layer, b, "V2"))
                    weigh(g, u, KT - 1)
                    if not lastb:
                        run_unit(layer, g + 1, 1 - u, "V3", unit(layer, b, "V3"))
                    o_unit(g, unit(layer, b, "O", last=lastb))

                each_batch(pe, layer, body)

            def transposes(m, tag):
                for t in range(TT):
                    pe.wait_ge(sem("xn_ready"), TT * m + t + 1)
                    for kc in range(KC):
                        last = nc.tensor.transpose(ps[:, 4 + kc, P * t:P * t + P], lnb[tag]["xn"][:, t, P * kc:P * kc + P],
                                                   ident[:, :])
                last.then_inc(sem("xnT_mm"), 1)
                pe.wait_ge(sem("xnT_ready"), m + 1)

            def q_projection(layer):
                for mt in range(2):
                    for kc in range(KC):
                        last = mm(ps[:, mt, :], wq[:, kc, P * mt:P * mt + P], lnb["mid"]["xnT"][:, kc, :],
                                  kc == 0, kc == KC - 1)
                last.then_inc(sem("q_mm"), 1)

            def out_projection(layer):
                pe.wait_ge(sem("oT_done"), B * (layer + 1))
                pe.wait_ge(sem("wo_in"), 16 * (layer + 1))
                for t in range(TT):
                    for e in range(2):
                        last = mm(ps[:, t // 2, D * (t % 2):D * (t % 2) + D], oT[:, e, P * t:P * t + P], wo[:, e, :],
                                  e == 0, e == 1)
                last.then_inc(sem("xo_mm"), 1)

            pe.wait_ge(sem("const_in"), 64)
            transposes(0, "mid")
            pe.wait_ge(sem("wq_in"), 16)
            pe.wait_ge(sem("const_ready"), 1)
            cross(0)
            out_projection(0)

            transposes(1, "mid")
            xnT = lnb["mid"]["xnT"]
            pe.wait_ge(sem("aw_in"), 16)
            pe.wait_ge(sem("x_cross"), 1)
            for t in range(TT):
                for kc in range(KC):
                    last = mm(ps[:, 6 + t // 2, D * (t % 2):D * (t % 2) + D], xnT[:, kc, P * t:P * t + P],
                              aw[:, 2, kc, :], kc == 0, kc == KC - 1)
            last.then_inc(sem("a_v_mm"), 1)
            for t in range(TT):
                for kc in range(KC):
                    last = mm(ps[:, t, :].rearrange("p (w c) -> p w c", w=2), xnT[:, kc, P * t:P * t + P],
                              aw[:, 0:2, kc, :], kc == 0, kc == KC - 1)
                last.then_inc(sem("a_qk_mm"), 1)
            pe.wait_ge(sem("a_qk"), TT)
            for t in range(TT):
                for r in (slice(0, 64), slice(64, 128)):
                    for c in range(DH):
                        last = mm(ps[r, 4, H * t:H * t + H], a_q[r, t, c, :, :].rearrange("p a f -> p (a f)"),
                                  a_k[r, t, c:D:DH], c == 0, c == DH - 1)
            last.then_inc(sem("a_e_mm"), 1)
            pe.wait_ge(sem("a_w_in"), 16 * B * H)
            pe.wait_ge(sem("a_v"), 1)
            for t in range(TT):
                for kc in range(KC):
                    last = nc.tensor.transpose(ps[:, 6 + kc, P * t:P * t + P], a_w[:, t, P * kc:P * kc + P],
                                               ident[:, :])
            last.then_inc(sem("a_wT_mm"), 1)
            pe.wait_ge(sem("a_wT"), 1)
            for t in range(TT):
                for kc in range(KC):
                    last = mm(ps[:, t // 2, D * (t % 2):D * (t % 2) + D], a_wT[:, kc, P * t:P * t + P],
                              aw[:, 3, kc, :], kc == 0, kc == KC - 1)
            last.then_inc(sem("a_z_mm"), 1)
            pe.wait_ge(sem("a_mT"), 1)
            for t in range(TT):
                last = nc.tensor.transpose(ps[:, 5, P * t:P * t + P], a_mT[:, t, :], ident[:, :])
            last.then_inc(sem("a_m_mm"), 1)
            pe.wait_ge(sem("a_m_ready"), 1)
            pe.wait_ge(sem("a_z"), 1)
            for t in range(TT):
                last = mm(ps[:, 2 + t // 2, D * (t % 2):D * (t % 2) + D], a_m[:, t, :], a_z[:, t, :], True, True)
            last.then_inc(sem("a_x_mm"), 1)

            transposes(2, "mid")
            f = lnb["mid"]
            pe.wait_ge(sem("wg_in"), 16)
            for t in range(TT):
                for kc in range(KC):
                    last = mm(ps[:, t // 2, D * (t % 2):D * (t % 2) + D], f["xnT"][:, kc, P * t:P * t + P],
                              wg[:, kc, :], kc == 0, kc == KC - 1)
            last.then_inc(sem("f_l_mm"), 1)
            pe.wait_ge(sem("fw_ready"), 2)
            pe.wait_ge(sem("xl_ready"), 1)
            pe.wait_ge(sem("ones16"), 1)
            for i in range(TT * E // 2):
                t, c = i // 4, slice(2 * D * (i % 4), 2 * D * (i % 4) + 2 * D)
                if i >= 4:
                    pe.wait_ge(sem("f_r"), 2 * (i - 3))
                o = ps[:, 4 + i % 4, :]
                if i == 0:
                    pe.wait_ge(sem("x_attn"), 1)
                mm(o, ones16[:, :], fbh[:, c], True, False)
                mm(o, ones16[:, :], fbl[:, c], False, False)
                for kc in range(KC):
                    for n, (a, w) in enumerate(((f["h"], fwh), (f["h"], fwl), (f["l"], fwh))):
                        last = mm(o, a[:, kc, P * t:P * t + P], w[:, kc, c], False, kc == KC - 1 and n == 2)
                last.then_inc(sem("f_mm"), 1)
            pe.wait_ge(sem("am_in"), 16)
            for k in range(1, 6):
                need(pe, "am_pow", k - 1)
                mm(ps[0:N, 2, 0:N], am[:, k - 1, 1, :], am[:, k - 1, 0, :], True, True)
                mm(ps[0:N, 3, 0:N], am[:, k - 1, 0, :], am[:, k - 1, 1, :], True, True).then_inc(sem("am_mm"), 1)

            pe.wait_ge(sem("mid_done"), 3)
            transposes(3, "mid")
            pe.wait_ge(sem("wq_in"), 32)
            cross(1)
            out_projection(1)

            transposes(4, "ssm")
            xnT = lnb["ssm"]["xnT"]
            pe.wait_ge(sem("ssm_in"), 32)
            for kc in range(KC):
                last = mm(ps[0:N, 2, :], bT[:, kc, :], xnT[:, kc, :], kc == 0, kc == KC - 1)
            last.then_inc(sem("u_mm"), 1)
            pe.wait_ge(sem("am_pow"), 5)
            for k in range(6):
                back = 1 << k
                pe.wait_ge(sem("scan"), k + 1)
                mm(ps[0:N, 3, 0:B * (NQ - back)], am[:, k, 1, :], st_s[:, :, 0:NQ - back], True,
                   True).then_inc(sem("scan_mm"), 1)
            pe.wait_ge(sem("scan"), 7)
            for t in range(TT):
                last = mm(ps[:, 6 + t // 2, D * (t % 2):D * (t % 2) + D],
                          st_s[:, 2 * t:2 * t + 2, :].rearrange("n b q -> n (b q)"), cT[:, :], True, True)
            last.then_inc(sem("y_mm"), 1)

            transposes(5, "moe")
            xnT = lnb["moe"]["xnT"]
            pe.wait_ge(sem("rw_in"), 32)
            for t in range(TT):
                for kc in range(KC):
                    last = mm(ps[:, 6, 2 * E * t:2 * E * t + 2 * E], xnT[:, kc, P * t:P * t + P],
                              rw[:, kc, :, :].rearrange("p r e -> p (r e)"), kc == 0, kc == KC - 1)
            last.then_inc(sem("r_mm"), 1)

            def scaled_transposes(i):
                pe.wait_ge(sem("xc_ready"), i + 1)
                if i >= 2:
                    pe.wait_ge(sem("xcl_ready"), i - 1)
                for t in range(TT):
                    for kc in range(KC):
                        last = nc.tensor.transpose(ps[:, 4 + 2 * (i % 2) + kc, P * t:P * t + P],
                                                   xc[:, i % 2, t, P * kc:P * kc + P], ident[:, :])
                last.then_inc(sem("xcT_mm"), 1)

            def router_down(it):
                pe.wait_ge(sem("inter"), it + 1)
                last = mm(ps[0:E, 4, :], rdw[:, it, :], i32[:, it % 2, :], it == 0, it == IT - 1)
                last.then_inc(sem("rd_mm"), 1)

            scaled_transposes(0)
            for w in range(2 * IT):
                it, r = w // 2, w % 2
                bank = 2 * (it % 2) + r
                if it >= 2:
                    pe.wait_ge(sem("inter"), it - 1)
                pe.wait_ge(sem("wlo_done"), w + 1)
                for e in range(E):
                    if it == 0:
                        if E * r + e + 1 < 2 * E:
                            scaled_transposes(E * r + e + 1)
                        pe.wait_ge(sem("xcl_ready"), E * r + e + 1)
                    for kc in range(KC):
                        c = (kc * E + e) * P
                        for n, (a, b_) in enumerate(((wh, xch), (wh, xcl), (wl, xch))):
                            last = mm(ps[:, bank, :], a[:, w % 2, c:c + P], b_[r][:, e, kc, :],
                                      e == 0 and kc == 0 and n == 0, e == E - 1 and kc == KC - 1 and n == 2)
                last.then_inc(sem("gu_mm"), 1)
                if r == 1 and it >= 1:
                    router_down(it - 1)
            router_down(IT - 1)
            pe.wait_ge(sem("ldT_ready"), 1)
            for t in range(TT):
                last = nc.tensor.transpose(ps[:, 5, E * t:E * t + E], ldT[:, P * t:P * t + P], ident[0:E, 0:E])
            last.then_inc(sem("ld_mm"), 1)
            for e in range(E):
                w = 2 * IT + e
                pe.wait_ge(sem("wlo_done"), w + 1)
                if e == 0:
                    pe.wait_ge(sem("ilo_done"), IT)
                    pe.wait_ge(sem("inter"), IT)
                if e >= 2:
                    pe.wait_ge(sem("y_added"), e - 1)
                for t in range(TT):
                    o = ps[:, 2 * (e % 2) + t // 2, D * (t % 2):D * (t % 2) + D]
                    for it in range(IT):
                        c = slice(D * it, D * it + D)
                        for n, (a, b_) in enumerate(((ih, wh), (ih, wl), (il, wh))):
                            last = mm(o, a[:, it, P * t:P * t + P], b_[:, w % 2, c], it == 0 and n == 0,
                                      it == IT - 1 and n == 2)
                last.then_inc(sem("d_mm"), 1)

        @block.scalar
        def _(act):
            def copy_T(m, tag, parts=False):
                act.wait_ge(sem("xnT_mm"), m + 1)
                if m == 1:
                    act.wait_ge(sem("qs_ready"), 1)
                nc.scalar.activation(lnb[tag]["xnT"][:, :, :], ps[:, 4:6, :], ACT.Copy).then_inc(sem("xnT_ready"), 1)
                if parts:
                    act.wait_ge(sem("xnT_ready"), m + 1)
                    nc.scalar.activation(lnb[tag]["h"][:, :, :], lnb[tag]["xnT"][:, :, :], ACT.Copy)\
                       .then_inc(sem("xh_ready"), 1)

            def split_kv(layer):
                act.wait_ge(sem(f"wkv{layer}_in"), 16)
                nc.scalar.activation(wkh[layer][:, :, :], wkv32[:, :, 0, :], ACT.Copy, scale=W_SCALE)
                nc.scalar.activation(wvh[layer][:, :, :], wkv32[:, :, 1, :], ACT.Copy, scale=W_SCALE)\
                   .then_inc(sem("kvh_ready"), 1)

            def split_ctx(g, u, h):
                k0, w = HALVES[h]
                act.wait_ge(sem(f"ctx_in{h}"), 16 * (g + 1))
                need(act, "v_mm", 4 * (g - 1))
                nc.scalar.activation(ch[u][:, :, k0:k0 + w], c32[:, h, :, 0:w], ACT.Copy).then_inc(sem("chi_done"), 1)

            def after_unit(layer, g, u, name, place):
                kind, i, s = name[0], int(name[1:] or 0), place[0]
                if kind == "K":
                    mt, (k0, w) = i // 2, HALVES[i % 2]
                    act.wait_ge(sem("k_mm"), 4 * g + i + 1)
                    need(act, "klo_done", 4 * g + i - 1)
                    o, src = k32[:, i % 2, 0:w], slot[s][:, 0:w]
                    if layer:
                        ins = nc.scalar.activation(o, src, ACT.Identity, scale=1 / W_SCALE, bias=bias[:, 1, mt:mt + 1])
                    else:
                        ins = nc.scalar.activation(o, src, ACT.Copy, scale=1 / W_SCALE)
                    ins.then_inc(sem("k32_done"), 1)
                elif kind == "V":
                    n = TILE_ROWS[V_TILES[i][0]] if i == 3 else P
                    kts = V_TILES[i]
                    act.wait_ge(sem("v_mm"), 4 * g + i + 1)
                    need(act, "pv_mm", 13 * (g - 1) + kts[-1] + 1)
                    nc.scalar.activation(v[0:n, kts[0]:kts[-1] + 1, :, 0:32],
                                         slot[s][0:n, 0:D * len(kts)].rearrange("p (k j c) -> p k j c", j=NP, c=32),
                                         ACT.Copy, scale=1 / W_SCALE).then_inc(sem("vhi_done"), 1)
                elif kind == "T":
                    act.wait_ge(sem("t_mm"), g + 1)
                    nc.scalar.activation(qcur[u][STACK:STACK + 1, :, :],
                                         slot[s][0:1, :].rearrange("p (j q) -> p j q", j=NP), ACT.Copy, scale=-1.0)\
                       .then_inc(sem("row_done"), 1)

            def cross(layer):
                g0 = B * layer
                act.wait_ge(sem("q_mm"), layer + 1)
                q = q32
                for mt in range(2):
                    if layer:
                        ins = nc.scalar.activation(q[:, mt, :], ps[:, mt, :], ACT.Identity, bias=bias[:, 0, mt:mt + 1])
                    else:
                        ins = nc.scalar.activation(q[:, mt, :], ps[:, mt, :], ACT.Copy)
                    ins.then_inc(sem("q32_done"), 1)

            def cross_first(layer):
                g0 = B * layer
                if layer == 0:
                    for h in range(2):
                        split_ctx(0, 0, h)
                for name in PROLOGUE_UNITS[:8]:
                    after_unit(layer, g0, 0, name, unit(layer, 0, name, prologue=True))
                if layer == 0:
                    for h in range(2):
                        split_ctx(1, 1, h)

            def cross_rest(layer):
                g0 = B * layer
                after_unit(layer, g0, 0, "T", unit(layer, 0, "T", prologue=True))

                def body(b, u):
                    g = g0 + b
                    lastb = isinstance(b, int) and b == B - 1
                    for k in range(KT):
                        n = TILE_ROWS[k]
                        for hb in range(2):
                            act.wait_ge(sem("main_mm"), 26 * g + 2 * k + hb + 1)
                            if hb == 0:
                                need(act, "plo_done", 13 * g + k - 1)
                                if k == 0 and isinstance(b, int) and b == 0:
                                    act.wait_ge(sem("qs_ready"), layer + 1)
                            nc.scalar.activation(p32[0:n, (u + k) % 2, BANK * hb:BANK * hb + BANK], ps[0:n, hb, :],
                                                 ACT.Exp, scale=DH ** -0.5).then_inc(sem("exp_done"), 1)
                        if not lastb:
                            for name in STEP_UNITS.get(k, []):
                                after_unit(layer, g + 1, 1 - u, name, unit(layer, b, name))
                        if k == 4 and not (layer == 1 and lastb):
                            for h in range(2):
                                split_ctx(g + 2, u, h)
                    if not lastb:
                        for name in ("T", "V2", "V3"):
                            after_unit(layer, g + 1, 1 - u, name, unit(layer, b, name))
                    s, _ = unit(layer, b, "O", last=lastb)
                    act.wait_ge(sem("o_mm"), g + 1)
                    for e in range(2):
                        o, src = oT[:, e, bass.ds(NQ * b, NQ)], slot[s][:, NQ * e:NQ * e + NQ]
                        if layer:
                            ins = nc.scalar.activation(o, src, ACT.Identity, bias=bias[:, 2, e:e + 1])
                        else:
                            ins = nc.scalar.activation(o, src, ACT.Copy)
                        if e == 1:
                            ins.then_inc(sem("oT_done"), 1)

                each_batch(act, layer, body)

            act.wait_ge(sem("const_in"), 64)
            split_kv(0)
            copy_T(0, "mid")
            cross_first(0)
            cross(0)
            cross_rest(0)

            act.wait_ge(sem("mid_free"), 1)
            copy_T(1, "mid")
            for t in range(2):
                act.wait_ge(sem("a_qk_mm"), t + 1)
                nc.scalar.activation(a_q[:, t, :, :, :], heads_by_dim(ps[:, t, 0:D]), ACT.Copy)
                nc.scalar.activation(a_k[:, t, :], ps[:, t, D:2 * D], ACT.Copy).then_inc(sem("a_qk"), 1)
            act.wait_ge(sem("a_max"), 1)
            for t in range(TT):
                ins = nc.scalar.activation(a_e[:, t, :], ps[:, 4, H * t:H * t + H], ACT.Exp, scale=DH ** -0.5,
                                           bias=a_s[:, 1, t:t + 1], accum_out=a_s[:, 2, t:t + 1])
            ins.then_inc(sem("a_exp"), 1)
            act.wait_ge(sem("a_wT_mm"), 1)
            nc.scalar.activation(a_wT[:, :, :], ps[:, 6:8, :], ACT.Copy).then_inc(sem("a_wT"), 1)
            act.wait_ge(sem("a_m_mm"), 1)
            nc.scalar.activation(a_m[:, :, :], ps[:, 5, :].rearrange("p (t c) -> p t c", t=TT), ACT.Copy)\
               .then_inc(sem("a_m_ready"), 1)

            copy_T(2, "mid", parts=True)
            act.wait_ge(sem("fw_in"), 32)
            nc.scalar.activation(fwh[:, :, :], fw32[:, :, :], ACT.Copy, scale=W_SCALE)
            nc.scalar.activation(fbh[:, :], fb32[:, :], ACT.Copy, scale=W_SCALE).then_inc(sem("fwh_ready"), 1)
            act.wait_ge(sem("f_m"), 1)
            for t in range(TT):
                ins = nc.scalar.activation(ex[:, t, :], lg[:, t, :], ACT.Exp, bias=f_s[:, 0, t:t + 1],
                                           accum_out=f_s[:, 1, t:t + 1])
            ins.then_inc(sem("f_e"), 1)
            act.wait_ge(sem("f_w"), 1)
            for i in range(TT * E // 2):
                act.wait_ge(sem("f_mm"), i + 1)
                for n in range(2):
                    q = 2 * i + n
                    e = 2 * (i % 4) + n
                    if q >= 4:
                        act.wait_ge(sem("f_add"), q - 3)
                    nc.scalar.activation(f_y[:, q % 4, :], ps[:, 4 + i % 4, D * n:D * n + D], ACT.Relu,
                                         scale=f_w[:, i // 4, e:e + 1]).then_inc(sem("f_r"), 1)
            split_kv(1)
            nc.scalar.nop().then_inc(sem("mid_done"), 1)

            act.wait_ge(sem("mid_done"), 3)
            copy_T(3, "mid")
            cross_first(1)
            cross(1)
            cross_rest(1)

            copy_T(4, "ssm")
            act.wait_ge(sem("u_mm"), 1)
            nc.scalar.activation(st_s[:, :, :], ps[0:N, 2, :].rearrange("n (b q) -> n b q", b=B), ACT.Copy)\
               .then_inc(sem("scan"), 1)
            act.wait_ge(sem("y_mm"), 1)
            nc.scalar.activation(g_a[:, :, :], ps[:, 6:8, :].rearrange("p b (t c) -> p (b t) c", t=2), ACT.Gelu)\
               .then_inc(sem("gelu"), 1)

            nc.scalar.nop().then_inc(sem("moe_free"), 1)
            act.wait_ge(sem("moe_free"), 3)
            for h in range(2):
                act.wait_ge(sem(f"ctx_in{h}"), 16 * (2 * B + 2))
            copy_T(5, "moe")

            def split_w(w):
                act.wait_ge(sem(f"w_in{w % 3}"), 16 * (w // 3 + 1))
                if w == 2 * IT or w == 2 * IT + 1:
                    act.wait_ge(sem("gu_mm"), w - 1)
                elif w > 2 * IT:
                    act.wait_ge(sem("d_mm"), w - 2 * IT - 1)
                elif w >= 2:
                    act.wait_ge(sem("gu_mm"), w - 1)
                nc.scalar.activation(wh[:, w % 2, :], w32[:, w % 3, :], ACT.Copy, scale=W_SCALE)\
                   .then_inc(sem("whi_done"), 1)

            def exp_gap(n):
                act.wait_ge(sem("r_top"), n + 1)
                lo, hi = (0, 2 * TT) if n == 0 else (2 * TT, 3 * TT)
                nc.scalar.activation(pr[:, lo:hi, 1:2], prt[:, lo:hi, 1:2], ACT.Exp).then_inc(sem("r_exp"), 1)

            def inner(it):
                act.wait_ge(sem("gu_mm"), 2 * it + 1)
                need(act, "inter", it)
                nc.scalar.activation(sg[:, 0, :], ps[:, 2 * (it % 2), :], ACT.Exp, scale=-1 / W_SCALE)\
                   .then_inc(sem("sg"), 1)
                act.wait_ge(sem("inter"), it + 1)
                nc.scalar.activation(ih[:, it, :], i32[:, it % 2, :], ACT.Copy).then_inc(sem("ihi_done"), 1)

            split_w(0)
            split_w(1)
            exp_gap(0)
            for i in range(2 * E):
                act.wait_ge(sem("xcT_mm"), i + 1)
                b_ = 4 + 2 * (i % 2)
                nc.scalar.activation(xch[i // E][:, i % E, :, :], ps[:, b_:b_ + 2, :], ACT.Copy)\
                   .then_inc(sem("xch_ready"), 1)
                if i == E:
                    split_w(2)
            for w in range(3, 2 * IT):
                split_w(w)
                if w % 2 == 1:
                    inner(w // 2 - 1)
            split_w(2 * IT)
            inner(IT - 1)
            act.wait_ge(sem("rd_mm"), IT)
            nc.scalar.activation(ldT[:, :], ps[0:E, 4, :], ACT.Copy).then_inc(sem("ldT_ready"), 1)
            split_w(2 * IT + 1)
            exp_gap(1)
            for e in range(2, E):
                split_w(2 * IT + e)

        @block.vector
        def _(dve):
            chained, powers = [0], [0]

            def link(ins):
                chained[0] += 1
                ins.then_inc(sem("dve_chain"), 1)
                dve.wait_ge(sem("dve_chain"), chained[0])

            def stats(tag, src):
                st, mv = lnb[tag]["st"], lnb[tag]["mv"]
                for t in range(TT):
                    ins = nc.vector.bn_stats(st[:, t, :], src[:, t, :])
                link(ins)
                for t in range(TT):
                    ins = nc.vector.bn_aggr(mv[:, t, :], st[:, t, :])
                link(ins)
                nc.vector.tensor_scalar(lnb[tag]["ve"][:, :].unsqueeze(2), mv[:, :, 1:2], LN_EPS, None, ALU.add)\
                  .then_inc(sem("var_ready"), 1)
                powers[0] += 1
                dve.wait_ge(sem("rstd_ready"), powers[0])

            def layernorm(tag, src, dst):
                stats(tag, src)
                mv, rstd = lnb[tag]["mv"], lnb[tag]["rstd"]
                for t in range(TT):
                    yield nc.vector.tensor_scalar(dst[:, t, :], src[:, t, :], mv[:, t, 0:1], rstd[:, t:t + 1],
                                                  ALU.subtract, ALU.mult)

            def norm_x(tag):
                for ins in layernorm(tag, x, lnb[tag]["xn"]):
                    ins.then_inc(sem("xn_ready"), 1)

            def split_kv(layer):
                dve.wait_ge(sem("kvh_ready"), layer + 1)
                for n, (hi, lo) in enumerate(((wkh, wkl), (wvh, wvl))):
                    ins = nc.vector.scalar_tensor_tensor(lo[layer][:, :, :], wkv32[:, :, n, :], W_SCALE,
                                                         hi[layer][:, :, :], ALU.mult, ALU.subtract)
                ins.then_inc(sem("kvw_ready"), 1)

            def split_ctx(g, u, h):
                k0, w = HALVES[h]
                dve.wait_ge(sem("chi_done"), 2 * g + h + 1)
                nc.vector.tensor_tensor(cl[u][:, :, k0:k0 + w], c32[:, h, :, 0:w], ch[u][:, :, k0:k0 + w],
                                        ALU.subtract).then_inc(sem("clo_done"), 1)

            def after_unit(layer, g, u, name, place):
                kind, i, s = name[0], int(name[1:] or 0), place[0]
                if kind == "K":
                    mt, (k0, w) = i // 2, HALVES[i % 2]
                    dve.wait_ge(sem("k32_done"), 4 * g + i + 1)
                    need(dve, f"stacked{mt}", 16 * 12 * g)
                    nc.vector.tensor_copy(kh[:, mt, k0:k0 + w], k32[:, i % 2, 0:w]).then_inc(sem("khi_done"), 1)
                    dve.sem_inc(sem(f"slot_freed{s}"), 1)
                elif kind == "V":
                    kts = V_TILES[i]
                    n = TILE_ROWS[kts[0]] if i == 3 else P
                    dve.wait_ge(sem("vhi_done"), 4 * g + i + 1)
                    nc.vector.scalar_tensor_tensor(
                        v[0:n, kts[0]:kts[-1] + 1, :, 33:65],
                        slot[s][0:n, 0:D * len(kts)].rearrange("p (k j c) -> p k j c", j=NP, c=32), 1 / W_SCALE,
                        v[0:n, kts[0]:kts[-1] + 1, :, 0:32], ALU.mult, ALU.subtract).then_inc(sem("vlo_done"), 1)
                    dve.wait_ge(sem("vlo_done"), 4 * g + i + 1)
                    dve.sem_inc(sem(f"slot_freed{s}"), 1)
                elif kind == "P":
                    j, h, w = i // 2, i % 2, HALVES[i % 2][1]
                    dve.wait_ge(sem("p_mm"), 16 * g + i + 1)
                    if i == 0:
                        need(dve, "m_ready", g)
                    nc.vector.reduce_max(mpart[:, j, h:h + 1], slot[s][:, 0:w], AX.X).then_inc(sem(f"slot_freed{s}"), 1)

            def max_ready(layer, g, place):
                s, used = place
                need(dve, f"slot_freed{s}", used)
                need(dve, f"slot_freed{1 - s}", used + s)
                nc.vector.tensor_tensor(m32[:, :].unsqueeze(2), mpart[:, :, 0:1], mpart[:, :, 1:2], ALU.max)\
                   .then_inc(sem("m32_done"), 1)
                dve.wait_ge(sem("m32_done"), g + 1)
                need(dve, "t_mm", g)
                nc.vector.tensor_scalar(m16[:, :], m32[:, :], 1 / M_SCALE, None, ALU.mult).then_inc(sem("m_ready"), 1)

            def take_queries(layer, g, b, u):
                need(dve, "main_mm", 26 * (g - 1))
                nc.vector.tensor_copy(qcur[u][0:STACK, :, :], qs[:, b, :, :]).then_inc(sem("qcur_ready"), 1)

            def normalise(g):
                dve.wait_ge(sem("pv_mm"), 13 * (g + 1))
                need(dve, "o_mm", g)
                nc.vector.reciprocal(rinv[:, :, :].unsqueeze(3), pvb[:, :, :, 32:33])
                for r, c in ((slice(0, 64), 0), (slice(64, 128), DH)):
                    ins = nc.vector.tensor_copy(osum[r, :, :, :], pvb[r, :, :, c:c + DH])
                ins.then_inc(sem("o_step"), 1)
                dve.wait_ge(sem("o_step"), 3 * g + 1)
                for r, c in ((slice(0, 64), 33), (slice(64, 128), 33 + DH)):
                    ins = nc.vector.tensor_tensor(onrm[r, :, :, :], osum[r, :, :, :], pvb[r, :, :, c:c + DH], ALU.add)
                ins.then_inc(sem("o_step"), 1)
                dve.wait_ge(sem("o_step"), 3 * g + 2)
                nc.vector.tensor_tensor(osum[:, :, :, :], onrm[:, :, :, :],
                                        rinv[:, :, :].unsqueeze(3).broadcast_to([P, 2, 4, DH]), ALU.mult)\
                   .then_inc(sem("o_step"), 1)
                dve.wait_ge(sem("o_step"), 3 * g + 3)
                nc.vector.tensor_copy(onrm[:, :, :, :], osum[:, :, :, :]).then_inc(sem("o_norm"), 1)

            def cross(layer):
                g0 = B * layer
                if layer == 0:
                    for h in range(2):
                        split_ctx(0, 0, h)
                dve.wait_ge(sem("v_ones"), layer + 1)
                for name in PROLOGUE_UNITS[:8]:
                    after_unit(layer, g0, 0, name, unit(layer, 0, name, prologue=True))
                dve.wait_ge(sem("q32_done"), 2 * (layer + 1))
                link(nc.vector.tensor_copy(qh[:, :, :], q32[:, :, :]))
                link(nc.vector.tensor_tensor(ql[:, :, :], q32[:, :, :], qh[:, :, :], ALU.subtract))
                for j in range(NP):
                    r, mt = slice(32 * (j % 4), 32 * (j % 4) + 32), j // 4
                    for side, c in ((0, slice(0, NQ)), (1, slice(NQ, P))):
                        for row, src in ((0, qh), (32, qh), (64, ql)):
                            ins = nc.vector.tensor_scalar(qs[row:row + 32, :, j, c],
                                                          src[r, mt, :].rearrange("p (b q) -> p b q", b=B),
                                                          small[r, SM_EVEN + side:SM_EVEN + side + 1], None, ALU.mult)
                ins.then_inc(sem("qs_ready"), 1)
                dve.wait_ge(sem("qs_ready"), layer + 1)
                take_queries(layer, g0, 0, 0)
                if layer == 0:
                    for h in range(2):
                        split_ctx(1, 1, h)
                for name in PROLOGUE_UNITS[8:24]:
                    after_unit(layer, g0, 0, name, unit(layer, 0, name, prologue=True))
                max_ready(layer, g0, unit(layer, 0, "T", prologue=True))
                slot_t = unit(layer, 0, "T", prologue=True)[0]
                dve.wait_ge(sem("row_done"), g0 + 1)
                dve.sem_inc(sem(f"slot_freed{slot_t}"), 1)

                def body(b, u):
                    g = g0 + b
                    lastb = isinstance(b, int) and b == B - 1
                    for k in range(KT):
                        n, buf = TILE_ROWS[k], (k + u) % PRING
                        if k == 0 and not lastb:
                            take_queries(layer, g + 1, b + 1, 1 - u)
                        dve.wait_ge(sem("exp_done"), 26 * g + 2 * k + 2)
                        need(dve, "pv_mm", 13 * g + k - ring_back(u, k) + 1)
                        nc.vector.tensor_copy(ph[0:n, buf, :], p32[0:n, (u + k) % 2, :]).then_inc(sem("phi_done"), 1)
                        if not lastb:
                            for name in STEP_UNITS.get(k, []):
                                after_unit(layer, g + 1, 1 - u, name, unit(layer, b, name))
                        if k == 4 and not (layer == 1 and lastb):
                            for h in range(2):
                                split_ctx(g + 2, u, h)
                    if not lastb:
                        max_ready(layer, g + 1, unit(layer, b, "T"))
                        dve.wait_ge(sem("row_done"), g + 2)
                        dve.sem_inc(sem(f"slot_freed{unit(layer, b, 'T')[0]}"), 1)
                        after_unit(layer, g + 1, 1 - u, "V2", unit(layer, b, "V2"))
                    normalise(g)
                    if not lastb:
                        after_unit(layer, g + 1, 1 - u, "V3", unit(layer, b, "V3"))
                    dve.wait_ge(sem("oT_done"), g + 1)
                    dve.sem_inc(sem(f"slot_freed{unit(layer, b, 'O', last=lastb)[0]}"), 1)

                each_batch(dve, layer, body)

                dve.wait_ge(sem("xo_mm"), layer + 1)
                o = ps[:, 0:2, :].rearrange("p b (t c) -> p (b t) c", t=2)
                link(nc.vector.tensor_tensor(x[:, :, :], x[:, :, :], o, ALU.add))
                if layer:
                    link(nc.vector.tensor_tensor(x[:, :, :], x[:, :, :],
                                                 rows[:, 2:3, :].broadcast_to([P, TT, D]), ALU.add))
                nc.vector.nop().then_inc(sem("x_cross"), 1)

            dve.wait_ge(sem("const_in"), 64)
            nc.vector.tensor_copy(ident16[:, :], ident[:, :]).then_inc(sem("const_ready"), 1)
            dve.wait_ge(sem("x_in"), 16)
            norm_x("mid")
            split_kv(0)
            cross(0)

            dve.wait_ge(sem("plo_done"), 13 * B)
            nc.vector.nop().then_inc(sem("mid_free"), 1)
            norm_x("mid")
            dve.wait_ge(sem("a_v_mm"), 1)
            nc.vector.tensor_copy(a_v[:, :, :], ps[:, 6:8, :].rearrange("p b (t c) -> p (b t) c", t=2))\
              .then_inc(sem("a_v"), 1)
            for t in range(2, TT):
                dve.wait_ge(sem("a_qk_mm"), t + 1)
                nc.vector.tensor_copy(a_q[:, t, :, :, :], heads_by_dim(ps[:, t, 0:D]))
                nc.vector.tensor_copy(a_k[:, t, :], ps[:, t, D:2 * D]).then_inc(sem("a_qk"), 1)
            dve.wait_ge(sem("a_e_mm"), 1)
            link(nc.vector.reduce_max(a_s[:, 0, :], ps[:, 4, 0:H * TT].rearrange("p (t c) -> p t c", t=TT), AX.X))
            nc.vector.tensor_scalar(a_s[:, 1, :], a_s[:, 0, :], -(DH ** -0.5), None, ALU.mult)\
              .then_inc(sem("a_max"), 1)
            dve.wait_ge(sem("a_exp"), 1)
            link(nc.vector.reciprocal(a_s[:, 3, :], a_s[:, 2, :]))
            link(nc.vector.tensor_tensor(a_p[:, :, :], a_e[:, :, :],
                                         a_s[:, 3, :].unsqueeze(2).broadcast_to([P, TT, H]), ALU.mult))
            for n in range(2):
                ins = nc.vector.tensor_tensor(
                    a_mT[:, :, NQ * n:NQ * n + NQ].rearrange("p t (h q) -> p t h q", q=4),
                    a_p[:, :, :].unsqueeze(3).broadcast_to([P, TT, H, 4]),
                    small[:, SM_MIX + 4 * n:SM_MIX + 4 * n + 4].unsqueeze(1).unsqueeze(1)
                    .broadcast_to([P, TT, H, 4]), ALU.mult)
            ins.then_inc(sem("a_mT"), 1)
            dve.wait_ge(sem("a_z_mm"), 1)
            nc.vector.tensor_copy(a_z[:, :, :], ps[:, 0:2, :].rearrange("p b (t c) -> p (b t) c", t=2))\
              .then_inc(sem("a_z"), 1)
            dve.wait_ge(sem("a_x_mm"), 1)
            o = ps[:, 2:4, :].rearrange("p b (t c) -> p (b t) c", t=2)
            link(nc.vector.tensor_tensor(x[:, :, :], x[:, :, :], o, ALU.add))
            link(nc.vector.tensor_tensor(x[:, :, :], x[:, :, :], rows[:, 0:1, :].broadcast_to([P, TT, D]), ALU.add))
            nc.vector.nop().then_inc(sem("x_attn"), 1)

            norm_x("mid")
            f = lnb["mid"]
            dve.wait_ge(sem("xh_ready"), 1)
            nc.vector.tensor_tensor(f["l"][:, :, :], f["xnT"][:, :, :], f["h"][:, :, :], ALU.subtract)\
              .then_inc(sem("xl_ready"), 1)
            dve.wait_ge(sem("fwh_ready"), 1)
            nc.vector.scalar_tensor_tensor(fwl[:, :, :], fw32[:, :, :], W_SCALE, fwh[:, :, :], ALU.mult,
                                           ALU.subtract).then_inc(sem("fw_ready"), 1)
            nc.vector.scalar_tensor_tensor(fbl[:, :], fb32[:, :], W_SCALE, fbh[:, :], ALU.mult,
                                           ALU.subtract).then_inc(sem("fw_ready"), 1)
            dve.wait_ge(sem("f_l_mm"), 1)
            o = ps[:, 0:2, :].rearrange("p b (t c) -> p (b t) c", t=2)
            link(nc.vector.tensor_tensor(lg[:, :, :], o, rows[:, 1:2, :].broadcast_to([P, TT, D]), ALU.add))
            link(nc.vector.reduce_max(f_s[:, 2, :], lg[:, :, :], AX.X))
            nc.vector.tensor_scalar(f_s[:, 0, :], f_s[:, 2, :], -1.0, None, ALU.mult).then_inc(sem("f_m"), 1)
            dve.wait_ge(sem("f_e"), 1)
            link(nc.vector.reciprocal(f_s[:, 2, :], f_s[:, 1, :]))
            for t in range(TT):
                ins = nc.vector.max(f_t[:, t, :], ex[:, t, :])
            link(ins)
            for t in range(TT):
                ins = nc.vector.max_index(f_i[:, t, :], f_t[:, t, :], ex[:, t, :])
            link(ins)
            link(nc.vector.tensor_scalar(f_m[:, :, :], f_i[:, :, 0:1], E - 1, None, ALU.bitwise_and))
            link(nc.vector.tensor_copy(f_f[:, :].unsqueeze(2), f_m[:, :, :]))
            link(nc.vector.tensor_scalar(f_s[:, 1, :], f_s[:, 2, :], 1 / W_SCALE, None, ALU.mult))
            link(nc.vector.tensor_tensor(f_s[:, 2, :], f_s[:, 1, :], f_t[:, :, 0], ALU.mult))
            for t in range(TT):
                ins = nc.vector.tensor_scalar(f_w[:, t, :], small[:, SM_IOTA:SM_IOTA + E], f_f[:, t:t + 1],
                                              f_s[:, 2, t:t + 1], ALU.is_equal, ALU.mult)
            ins.then_inc(sem("f_w"), 1)
            for q in range(TT * E):
                t = q // E
                dve.wait_ge(sem("f_r"), q + 1)
                need(dve, "f_add", q)
                nc.vector.tensor_tensor(x[:, t, :], x[:, t, :], f_y[:, q % 4, :], ALU.add).then_inc(sem("f_add"), 1)
            dve.wait_ge(sem("f_add"), TT * E)
            for k in range(1, 6):
                dve.wait_ge(sem("am_mm"), k)
                nc.vector.tensor_copy(am[:, k, :, :], ps[0:N, 2:4, 0:N]).then_inc(sem("am_pow"), 1)
            split_kv(1)
            nc.vector.nop().then_inc(sem("mid_done"), 1)
            norm_x("mid")
            dve.wait_ge(sem("xn_ready"), 4 * TT)
            nc.vector.nop().then_inc(sem("mid_done"), 1)

            cross(1)

            dve.wait_ge(sem("plo_done"), 2 * 13 * B)
            norm_x("ssm")
            for k in range(6):
                back = 1 << k
                dve.wait_ge(sem("scan_mm"), k + 1)
                nc.vector.tensor_tensor(st_s[:, :, back:NQ], st_s[:, :, back:NQ],
                                        ps[0:N, 3, 0:B * (NQ - back)].rearrange("n (b q) -> n b q", b=B),
                                        ALU.add).then_inc(sem("scan"), 1)
            dve.wait_ge(sem("gelu"), 1)
            for ins in layernorm("ssm", g_a, g_n):
                pass
            link(ins)
            link(nc.vector.tensor_tensor(g_a[:, :, :], g_n[:, :, :], rows[:, 3:4, :].broadcast_to([P, TT, D]), ALU.mult))
            link(nc.vector.tensor_tensor(g_n[:, :, :], g_a[:, :, :], rows[:, 4:5, :].broadcast_to([P, TT, D]), ALU.add))
            link(nc.vector.memset(g_z[:, :, :], 0.0))
            link(nc.vector.tensor_tensor(g_m[:, :, :], g_n[:, :, :], g_n[:, :, :], ALU.subtract))
            link(nc.vector.tensor_scalar(g_f[:, :, :], g_m[:, :, :], 0.0, None, ALU.is_equal))
            link(nc.vector.copy_predicated(g_z[:, :, :], g_f[:, :, :], g_n[:, :, :]))
            link(nc.vector.tensor_scalar(g_m[:, :, :], g_n[:, :, :], F32_MAX, CLAMP, ALU.is_gt, ALU.mult))
            link(nc.vector.tensor_tensor(g_z[:, :, :], g_z[:, :, :], g_m[:, :, :], ALU.add))
            link(nc.vector.tensor_scalar(g_m[:, :, :], g_n[:, :, :], -F32_MAX, -CLAMP, ALU.is_lt, ALU.mult))
            link(nc.vector.tensor_tensor(g_z[:, :, :], g_z[:, :, :], g_m[:, :, :], ALU.add))
            link(nc.vector.tensor_tensor(x[:, :, :], x[:, :, :], g_z[:, :, :], ALU.add))
            nc.vector.nop().then_inc(sem("moe_free"), 2)

            for h in range(2):
                dve.wait_ge(sem(f"ctx_in{h}"), 16 * (2 * B + 2))
            dve.wait_ge(sem("moe_free"), 3)
            norm_x("moe")
            xn = lnb["moe"]["xn"]

            def split_w(w):
                dve.wait_ge(sem("whi_done"), w + 1)
                nc.vector.scalar_tensor_tensor(wl[:, w % 2, :], w32[:, w % 3, :], W_SCALE, wh[:, w % 2, :],
                                               ALU.mult, ALU.subtract).then_inc(sem("wlo_done"), 1)

            def top2(lo, hi, n):
                for i in range(lo, hi):
                    ins = nc.vector.max(top[:, i, :], lgm[:, i, :])
                link(ins)
                for i in range(lo, hi):
                    ins = nc.vector.max_index(topi[:, i, :], top[:, i, :], lgm[:, i, :])
                link(ins)
                nc.vector.tensor_copy(topf[:, lo:hi, :], topi[:, lo:hi, 0:2])
                nc.vector.tensor_tensor(prt[:, lo:hi, 1:2], top[:, lo:hi, 1:2], top[:, lo:hi, 0:1], ALU.subtract)\
                  .then_inc(sem("r_top"), 1)
                dve.wait_ge(sem("r_exp"), n + 1)
                link(nc.vector.tensor_scalar(prt[:, lo:hi, 0:1], pr[:, lo:hi, 1:2], 1.0, None, ALU.add))
                link(nc.vector.reciprocal(pr[:, lo:hi, 0:1], prt[:, lo:hi, 0:1]))
                link(nc.vector.tensor_tensor(prt[:, lo:hi, 1:2], pr[:, lo:hi, 1:2], pr[:, lo:hi, 0:1], ALU.mult))
                for i in range(lo, hi):
                    nc.vector.tensor_scalar(cmb[:, i, :], small[:, SM_IOTA:SM_IOTA + E], topf[:, i, 0:1],
                                            pr[:, i, 0:1], ALU.is_equal, ALU.mult)
                    ins = nc.vector.tensor_scalar(cmb2[:, i, :], small[:, SM_IOTA:SM_IOTA + E], topf[:, i, 1:2],
                                                  prt[:, i, 1:2], ALU.is_equal, ALU.mult)
                link(ins)
                link(nc.vector.tensor_tensor(cmb[:, lo:hi, :], cmb[:, lo:hi, :], cmb2[:, lo:hi, :], ALU.add))

            split_w(0)
            split_w(1)
            dve.wait_ge(sem("r_mm"), 1)
            link(nc.vector.tensor_copy(
                lgm[:, 0:2 * TT, :].rearrange("p (r t) e -> p r t e", r=2),
                ps[:, 6, 0:2 * E * TT].rearrange("p (t r e) -> p r t e", r=2, e=E)))
            top2(0, 2 * TT, 0)

            def scale_tokens(i):
                r, e = i // E, i % E
                if i >= 2:
                    dve.wait_ge(sem("xcT_mm"), i - 1)
                for t in range(TT):
                    ins = nc.vector.tensor_scalar(xc[:, i % 2, t, :], xn[:, t, :], cmb[:, TT * r + t, e:e + 1], None,
                                                  ALU.mult)
                ins.then_inc(sem("xc_ready"), 1)

            scale_tokens(0)
            for i in range(2 * E):
                if i + 1 < 2 * E:
                    scale_tokens(i + 1)
                dve.wait_ge(sem("xch_ready"), i + 1)
                b_ = 4 + 2 * (i % 2)
                nc.vector.tensor_tensor(xcl[i // E][:, i % E, :, :], ps[:, b_:b_ + 2, :], xch[i // E][:, i % E, :, :],
                                        ALU.subtract).then_inc(sem("xcl_ready"), 1)
                if i == E:
                    split_w(2)
            for it in range(IT):
                if it < IT - 1:
                    split_w(2 * it + 3)
                g_ps, u_ps = ps[:, 2 * (it % 2), :], ps[:, 2 * (it % 2) + 1, :]
                dve.wait_ge(sem("sg"), it + 1)
                link(nc.vector.tensor_scalar(sg[:, 1, :], sg[:, 0, :], 1.0, None, ALU.add))
                link(nc.vector.reciprocal(sg[:, 2, :], sg[:, 1, :]))
                link(nc.vector.tensor_tensor(sg[:, 1, :], sg[:, 2, :], g_ps, ALU.mult))
                dve.wait_ge(sem("gu_mm"), 2 * it + 2)
                if it >= 2:
                    dve.wait_ge(sem("ilo_done"), it - 1)
                    dve.wait_ge(sem("rd_mm"), it - 1)
                nc.vector.scalar_tensor_tensor(i32[:, it % 2, :], u_ps, 1 / (W_SCALE * W_SCALE), sg[:, 1, :],
                                               ALU.mult, ALU.mult).then_inc(sem("inter"), 1)
                if it < IT - 1:
                    split_w(2 * it + 4)
            split_w(2 * IT + 1)
            dve.wait_ge(sem("ld_mm"), 1)
            link(nc.vector.tensor_copy(lgm[:, 2 * TT:3 * TT, :],
                                       ps[:, 5, 0:E * TT].rearrange("p (t e) -> p t e", t=TT)))
            top2(2 * TT, 3 * TT, 1)
            link(nc.vector.tensor_scalar(cmb2[:, 2 * TT:3 * TT, :], cmb[:, 2 * TT:3 * TT, :], 1 / W_SCALE, None,
                                         ALU.mult))
            for e in range(E):
                dve.wait_ge(sem("d_mm"), e + 1)
                if e + 2 < E:
                    split_w(2 * IT + e + 2)
                need(dve, "y_added", e)
                for t in range(TT):
                    o = ps[:, 2 * (e % 2) + t // 2, D * (t % 2):D * (t % 2) + D]
                    ins = nc.vector.scalar_tensor_tensor(x[:, t, :], o, cmb2[:, 2 * TT + t, e:e + 1], x[:, t, :],
                                                         ALU.mult, ALU.add)
                ins.then_inc(sem("y_added"), 1)
            dve.wait_ge(sem("y_added"), E)
            nc.vector.nop().then_inc(sem("x_final"), 1)


def lay_out(a):
    def chunks(w):
        return w.reshape(-1, P, w.shape[1]).transpose(1, 0, 2)

    d = {}
    d["x"] = a["x"].reshape(TT, P, D).transpose(1, 0, 2)
    d["ctxT"] = a["ctx_1024"].transpose(0, 2, 1).reshape(B, KC, P, S).transpose(0, 2, 1, 3)
    d["wkv"] = np.stack([np.stack([chunks(a[f"L{i}_xattn_Wk"].T), chunks(a[f"L{i}_xattn_Wv"].T)], 2) for i in range(2)])
    d["wq"] = np.stack([chunks(a[f"L{i}_xattn_Wq"].T) for i in range(2)])
    d["wo"] = np.stack([a[f"L{i}_xattn_Wo"].T.reshape(NP, 2, DH, D).transpose(0, 2, 1, 3).reshape(P, 2, D)
                        for i in range(2)])
    d["aw"] = np.stack([chunks(a[f"L0_attn_W{n}"]) for n in "qkvo"], 1)
    d["bias"] = np.stack([a["L1_xattn_bq"].reshape(2, P).T, a["L1_xattn_bk"].reshape(2, P).T,
                          a["L1_xattn_bv"].reshape(NP, 2, DH).transpose(0, 2, 1).reshape(P, 2)], 1)
    rows = np.stack([a["L0_attn_bo"], a["L0_ffn_bg"], a["L1_xattn_bo"], a["L1_attn_gamma"], a["L1_attn_beta"]])
    d["rows"] = np.broadcast_to(rows, (P, 5, D))
    d["fw"] = a["L0_ffn_We"].transpose(1, 0, 2).reshape(KC, P, E * D).transpose(1, 0, 2)
    d["fb"] = a["L0_ffn_be"].reshape(1, E * D)
    d["wg"] = chunks(a["L0_ffn_Wg"])
    d["am"] = np.stack([a["L1_attn_A"], a["L1_attn_A"].T], 1)
    d["bT"] = chunks(a["L1_attn_B"].T)
    d["cT"] = a["L1_attn_C"].T
    d["rw"] = np.stack([chunks(a["L1_ffn_router_gate"].T), chunks(a["L1_ffn_router_up"].T)], 2)
    d["rdw"] = chunks(a["L1_ffn_router_down"].T)
    gu = np.stack([a["L1_ffn_w_gate"], a["L1_ffn_w_up"]])
    d["wgu"] = gu.reshape(2, E, IT, P, KC, P).transpose(2, 0, 5, 4, 1, 3).reshape(2 * IT, P, KC * E * P)
    d["wd"] = a["L1_ffn_w_down"].reshape(E, D, IT, P).transpose(0, 3, 2, 1).reshape(E, P, IT * D)
    d["ident"] = np.eye(P, dtype=np.float32)
    small = np.zeros((P, 24), np.float32)
    small[:, 0] = np.arange(P) % 32 < DH
    small[:, 1] = np.arange(P) % 32 >= DH
    small[:, 2:2 + E] = np.arange(E)
    for n in range(2):
        for q in range(4):
            small[:, 10 + 4 * n + q] = (np.arange(P) // NQ == n) & (np.arange(P) % 4 == q)
    d["small"] = small
    d["ones"] = np.full((1, NP, S), M_SCALE, np.float16)
    return {k: np.ascontiguousarray(w) for k, w in d.items()}


def kernel(**inputs):
    import concourse.bacc as bacc
    from concourse.bass_utils import run_bass_kernel_spmd

    arrays = lay_out({k: np.asarray(w) for k, w in inputs.items()})
    nc = bacc.Bacc("TRN2", target_bir_lowering=False, num_devices=1)
    d = {k: nc.dram_tensor(f"in_{k}", w.shape, mybir.dt.from_np(w.dtype), kind="ExternalInput").ap()
         for k, w in arrays.items()}
    d["scratch"] = nc.dram_tensor("scratch", (T, D), F32, kind="Internal").ap()
    out = nc.dram_tensor("out", (T, D), F32, kind="ExternalOutput").ap()
    build(nc, d, out.rearrange("(t p) c -> p t c", p=P))
    r = run_bass_kernel_spmd(nc, [{f"in_{k}": w for k, w in arrays.items()}], core_ids=[0])
    return r.results[0]["out"].reshape(B, NQ, D)
```

```python
from contextlib import ExitStack

import concourse.bass as bass
import numpy as np
from concourse import mybir

F32 = mybir.dt.float32
F16 = mybir.dt.float16
U32 = mybir.dt.uint32
ALU = mybir.AluOpType
ACT = mybir.ActivationFunctionType
AX = mybir.AxisListType

P = 128
D = 256
KC = D // P
B = 8
NQ = 64
T = B * NQ
TT = T // P
H = 16
DH = D // H
NP = H // 2
S = 1601
KT = -(-S // P)
HALF = (S + 1) // 2
E = 8
FI = 1024
IT = FI // P
N = 64
BANK = 512
STACK = 96
VW = 65
W_SCALE = 256.0
M_SCALE = 64.0
LN_EPS = 1e-5
F32_MAX = 3.4028234663852886e38
CLAMP = 1e6

HALVES = [(0, HALF), (HALF, S - HALF)]
TILE_ROWS = [min(P, S - P * k) for k in range(KT)]
QUARTERS = [(0, HALF - HALF // 2), (HALF - HALF // 2, HALF // 2), (HALF, HALF // 2), (HALF + HALF // 2, HALF // 2)]
QW = QUARTERS[0][1]
V_TILES = [range(2 * v, min(2 * v + 2, KT)) for v in range((KT + 1) // 2)]
K_UNITS, V_UNITS = 8, len(V_TILES)
PRING = 4

PROLOGUE_UNITS = ("K0 K1 K2 K3 Q K4 K5 K6 P0 P1 K7 P2 P3 V0 P4 P5 V1 P6 P7 P8 P9 P10 P11 P12 P13 P14 P15 T "
                  "N0 N1 N2 N3").split()
STEP_UNITS = {0: ["V2", "P0", "S", "W"],
              1: ["S", "P1", "V3", "P2", "W"],
              2: ["S", "V4", "P3", "W"],
              3: ["S", "V5", "P4", "W"],
              4: ["S", "O", "K4", "P5", "W"],
              5: ["V6", "S", "K5", "P6", "W"],
              6: ["S", "P7", "K6", "P8", "W"],
              7: ["S", "K7", "P9", "W"],
              8: ["S", "V0", "P10", "W"],
              9: ["S", "V1", "P11", "W"],
              10: ["S", "N0", "P12", "W"],
              11: ["S", "P13", "N1", "P14", "W"],
              12: ["S", "P15", "N2", "W", "T", "N3"]}
OWN_UNITS = ("V2", "V3", "V4", "V5", "V6")
CTX_STEPS = {4: 0, 6: 1, 8: 2, 10: 3}
LAG = 3
READ_BY = {"K": ("khi_done", K_UNITS), "N": ("khi_done", K_UNITS), "V": ("vlo_done", V_UNITS),
           "P": ("max_done", 2 * NP), "T": ("row_done", 1), "O": ("oT_done", 1)}


def prob_buffer(u, k):
    step = KT * u + k
    return step % PRING if step < 20 else (step - 20) % 3


def place(name, kind):
    if name[0] in "KNV":
        return int(name[1:]) % 2
    return 3 if kind == "prologue" and name[0] == "P" and int(name[1:]) % 2 else 2


def pair_and_half(i):
    return (i // 2, i % 2) if i < NP else (NP // 2 + i % (NP // 2), (i - NP) // (NP // 2))


def exp_buffer(u, k):
    step = KT * u + k
    return step % 3 if step < 24 else step - 24


def steps_back(buffer, u, k):
    at = KT * u + k
    for back in range(1, 2 * KT):
        s = (at - back) % (2 * KT)
        if buffer(s // KT, s % KT) == buffer(u, k):
            return back
    raise AssertionError


def has_unit(kind, name):
    if name in ("S", "W") or name in OWN_UNITS:
        return True
    if name == "O":
        return kind != "first"
    if name[0] == "N":
        return kind in ("first", "inner")
    return kind != "last"


def batches_ahead(kind, name):
    if kind in ("prologue", "end"):
        return 1 if name[0] == "N" else 0
    return 0 if name in OWN_UNITS else {"O": -1, "N": 2}.get(name[0], 1)


def build(nc, d, out):
    with ExitStack() as ctx:
        def sb(stack, name, shape, dt=F32):
            return stack.enter_context(nc.sbuf_tensor(name, shape, dt))

        sems = {}

        def sem(name):
            if name not in sems:
                sems[name] = ctx.enter_context(nc.semaphore(name))
            return sems[name]

        def need(eng, name, value):
            if isinstance(value, int) and value <= 0:
                return
            eng.wait_ge(sem(name), value)

        x = sb(ctx, "x", [P, TT, D])
        oT = sb(ctx, "oT", [P, 2, T])
        wkv32 = sb(ctx, "wkv32", [P, KC, 2, D])
        wkh = [sb(ctx, f"wkh{i}", [P, KC, D], F16) for i in range(2)]
        wkl = [sb(ctx, f"wkl{i}", [P, KC, D], F16) for i in range(2)]
        wvh = [sb(ctx, f"wvh{i}", [P, KC, D], F16) for i in range(2)]
        wvl = [sb(ctx, f"wvl{i}", [P, KC, D], F16) for i in range(2)]
        wq = sb(ctx, "wq", [P, KC, D])
        wo = sb(ctx, "wo", [P, 2, D])
        ident = sb(ctx, "ident", [P, P])
        ident16 = sb(ctx, "ident16", [P, P], F16)
        small = sb(ctx, "small", [P, 24])
        bias = sb(ctx, "bias", [P, 3, 2])
        rows = sb(ctx, "rows", [P, 5, D])
        am = sb(ctx, "am", [N, 6, 2, N])
        half = sb(ctx, "half", [P, TT])
        SM_EVEN, SM_IOTA, SM_MIX = 0, 2, 10

        lnb = {}

        def ln_buffers(stack, tag):
            lnb[tag] = dict(
                xn=sb(stack, f"xn_{tag}", [P, TT, D]), xnT=sb(stack, f"xnT_{tag}", [P, KC, T]),
                h=sb(stack, f"xh_{tag}", [P, KC, T], F16), l=sb(stack, f"xl_{tag}", [P, KC, T], F16),
                st=sb(stack, f"st_{tag}", [P, TT, 6]), mv=sb(stack, f"mv_{tag}", [P, TT, 2]),
                ve=sb(stack, f"ve_{tag}", [P, TT]), rstd=sb(stack, f"rs_{tag}", [P, TT]))

        with ExitStack() as s:
            ln_buffers(s, "moe")
            xch = [sb(s, f"xch{r}", [P, E, KC, T], F16) for r in range(2)]
            xcl = [sb(s, f"xcl{r}", [P, E, KC, T], F16) for r in range(2)]
            w32 = sb(s, "w32", [P, 3, KC * E * P])
            wh = sb(s, "wh", [P, 2, KC * E * P], F16)
            wl = sb(s, "wl", [P, 2, KC * E * P], F16)
            xc = sb(s, "xc", [P, 2, TT, D])
            ih = sb(s, "ih", [P, IT, T], F16)
            il = sb(s, "il", [P, IT, T], F16)
            i32 = sb(s, "i32", [P, 2, T])
            sg = sb(s, "sg", [P, 3, T])
            rw = sb(s, "rw", [P, KC, 2, E])
            rdw = sb(s, "rdw", [P, IT, E])
            ldT = sb(s, "ldT", [E, T])
            lgm = sb(s, "lgm", [P, 3 * TT, E])
            top = sb(s, "top", [P, 3 * TT, 8])
            topi = sb(s, "topi", [P, 3 * TT, 8], U32)
            topf = sb(s, "topf", [P, 3 * TT, 2])
            pr = sb(s, "pr", [P, 3 * TT, 2])
            prt = sb(s, "prt", [P, 3 * TT, 2])
            cmb = sb(s, "cmb", [P, 3 * TT, E])
            cmb2 = sb(s, "cmb2", [P, 3 * TT, E])
        c32 = sb(ctx, "c32", [P, 2, KC, HALF])
        ch = [sb(ctx, f"ch{i}", [P, KC, S], F16) for i in range(2)]
        cl = [sb(ctx, f"cl{i}", [P, KC, S], F16) for i in range(2)]
        with ExitStack() as s:
            ln_buffers(s, "mid")
            q32 = sb(s, "q32", [P, 2, T])
            qh = sb(s, "qh", [P, 2, T], F16)
            ql = sb(s, "ql", [P, 2, T], F16)
            aw = sb(s, "aw", [P, 4, KC, D])
            a_q = sb(s, "a_q", [P, TT, DH, H, 4])
            a_k = sb(s, "a_k", [P, TT, D])
            a_v = sb(s, "a_v", [P, TT, D])
            a_w = sb(s, "a_w", [P, TT, D])
            a_wT = sb(s, "a_wT", [P, KC, T])
            a_z = sb(s, "a_z", [P, TT, D])
            a_e = sb(s, "a_e", [P, TT, H])
            a_p = sb(s, "a_p", [P, TT, H])
            a_mT = sb(s, "a_mT", [P, TT, P])
            a_m = sb(s, "a_m", [P, TT, P])
            a_s = sb(s, "a_s", [P, 4, TT])
            fw32 = sb(s, "fw32", [P, KC, E * D])
            fwh = sb(s, "fwh", [P, KC, E * D], F16)
            fwl = sb(s, "fwl", [P, KC, E * D], F16)
            fb32 = sb(s, "fb32", [1, E * D])
            fbh = sb(s, "fbh", [1, E * D], F16)
            fbl = sb(s, "fbl", [1, E * D], F16)
            ones16 = sb(s, "ones16", [1, P], F16)
            wg = sb(s, "wg", [P, KC, D])
            lg = sb(s, "lg", [P, TT, D])
            ex = sb(s, "ex", [P, TT, D])
            f_s = sb(s, "f_s", [P, 3, TT])
            f_t = sb(s, "f_t", [P, TT, 8])
            f_i = sb(s, "f_i", [P, TT, 8], U32)
            f_m = sb(s, "f_m", [P, TT, 1], U32)
            f_f = sb(s, "f_f", [P, TT])
            f_w = sb(s, "f_w", [P, TT, E])
            f_y = sb(s, "f_y", [P, 4, D])
        with ExitStack() as s:
            ln_buffers(s, "ssm")
            bT = sb(s, "bT", [P, KC, N])
            cT = sb(s, "cT", [N, D])
            st_s = sb(s, "st_s", [N, B, NQ])
            g_a = sb(s, "g_a", [P, TT, D])
            g_n = sb(s, "g_n", [P, TT, D])
            g_m = sb(s, "g_m", [P, TT, D])
            g_z = sb(s, "g_z", [P, TT, D])
            g_f = sb(s, "g_f", [P, TT, D], U32)
        p32 = sb(ctx, "p32", [P, 3, H * NQ])
        ph = sb(ctx, "ph", [P, PRING, H * NQ], F16)
        pl = sb(ctx, "pl", [P, PRING, H * NQ], F16)
        qs = sb(ctx, "qs", [STACK, NP, B, P], F16)
        qbh = sb(ctx, "qbh", [P, 2, B, 2, NQ], F16)
        qbl = ph[:, 0:2, :].rearrange("p m (b h q) -> p m b h q", b=B, h=2)
        qbcur = sb(ctx, "qbcur", [P, 2, P], F16)
        qcur = [sb(ctx, f"qcur{i}", [STACK + 1, NP, P], F16) for i in range(2)]
        ks = [sb(ctx, f"ks{i}", [STACK + 1, NP, S], F16) for i in range(2)]
        k32 = sb(ctx, "k32", [P, 4, QW])
        kh = sb(ctx, "kh", [P, 2, S], F16)
        kl = sb(ctx, "kl", [P, 2, S], F16)
        v = sb(ctx, "v", [P, KT, NP, VW], F16)
        mpart = sb(ctx, "mpart", [P, NP, 2])
        m32 = sb(ctx, "m32", [P, NP])
        m16 = sb(ctx, "m16", [P, NP], F16)
        rinv = sb(ctx, "rinv", [P, 2, 4])
        osum = sb(ctx, "osum", [P, 2, 4, DH])
        opart = sb(ctx, "opart", [P, 2, 4, DH])

        ps = ctx.enter_context(nc.psum_tensor("ps", [P, 8, BANK], F32))
        flat = ps[:, :, :].rearrange("p b c -> p (b c)")
        slot = [flat[:, 2048:2560], flat[:, 2560:3072], flat[:, 3072:4096], flat[:, 1024:2048]]
        pvb = ps[:, 2:4, 0:4 * VW].rearrange("p b (j c) -> p b j c", c=VW)

        block = ctx.enter_context(nc.Block())

        def kind_of(b):
            return {0: "first", B - 2: "next_to_last", B - 1: "last"}.get(b, "inner") if isinstance(b, int) else "inner"

        def units(kind):
            if kind == "prologue":
                return [n for n in PROLOGUE_UNITS if n != "Q"]
            if kind == "end":
                return ["O"]
            return [n for k in range(KT) for n in STEP_UNITS[k] if n not in ("S", "W") and has_unit(kind, n)]

        def last_use(kind, g, name):
            def signal(kind_, g_, n):
                sem_name, per = READ_BY[n[0]]
                return sem_name, per * (g_ + batches_ahead(kind_, n)) + int(n[1:] or 0) + 1

            def shared(names, kind_):
                return [n for n in names if place(n, kind_) == place(name, kind)]

            earlier = shared(units(kind)[:units(kind).index(name)], kind)
            if earlier:
                return signal(kind, g, earlier[-1])
            before = {"first": "prologue", "inner": "inner", "next_to_last": "inner", "last": "next_to_last",
                      "end": "last"}
            if kind == "prologue":
                return None
            g_ = g if kind in ("first", "end") else g - 1
            return signal(before[kind], g_, shared(units(before[kind]), before[kind])[-1])

        def heads_by_dim(q):
            return q.rearrange("p (a c) -> p c a", a=H).unsqueeze(3).broadcast_to([P, DH, H, 4])

        def each_batch(eng, layer, body):
            body(0, 0)
            with eng.Fori(0, (B - 4) // 2) as i:
                body(2 * i + 1, 1)
                body(2 * i + 2, 0)
            for b in range(B - 3, B):
                body(b, b % 2)

        @block.sync
        def _(sp):
            def load(dst, src, name):
                sp.dma_start(dst, src).then_inc(sem(name), 16)

            def load_ctx(g, b):
                for h, (k0, w) in enumerate(HALVES):
                    need(sp, "clo_done", 4 * g + 2 * h - 2)
                    load(c32[:, h, :, 0:w], d["ctxT"][b, :, :, k0:k0 + w], f"ctx_in{h}")

            def restack(g, u, mts=(0, 1)):
                for mt in mts:
                    sp.wait_ge(sem("klo_done"), K_UNITS * g + 4 * mt + 4)
                    if mt == mts[0]:
                        need(sp, "main_mm", 2 * KT * (g - 1) + 1)
                    for j in range(4):
                        r, pair = slice(32 * j, 32 * j + 32), 4 * mt + j
                        load(ks[u][0:32, pair, :], kh[r, mt, :], f"stacked{mt}")
                        load(ks[u][32:64, pair, :], kl[r, mt, :], f"stacked{mt}")
                        load(ks[u][64:96, pair, :], kh[r, mt, :], f"stacked{mt}")

            def store_parts(g, u):
                sp.wait_ge(sem("clo_done"), 4 * g + 4)
                for part, c in enumerate((ch, cl)):
                    load(d["cparts"][g, part], c[u][:, :, :], f"parts_stored{u}")

            def load_parts(g, b, u):
                for h in range(2):
                    need(sp, f"parts_in{h}", 32 * (g - B))
                for h, (k0, w) in enumerate(HALVES):
                    sp.wait_ge(sem("v_mm"), V_UNITS * (g - 2) + (4 if h == 0 else V_UNITS))
                    for part, c in enumerate((ch, cl)):
                        load(c[u][:, :, k0:k0 + w], d["cparts"][b, part, :, :, k0:k0 + w], f"parts_in{h}")

            load(x[:, :, :], d["x"], "x_in")
            for layer in range(2):
                if layer == 0:
                    load(wkv32[:, :, :, :], d["wkv"][0], "wkv0_in")
                    load_ctx(0, 0)
                    load_ctx(1, 1)
                else:
                    sp.wait_ge(sem("mid_done"), 3)
                g0 = B * layer
                for u in range(2):
                    load(ks[u][STACK:STACK + 1, :, :], d["ones"], "ones_in")
                restack(g0, 0, (0,))
                sp.wait_ge(sem("qb_ready"), layer + 1)
                load(d["qscratch"][0], qbh[:, :, :, :, :].rearrange("p m b h q -> p m (b h q)"), "q_out")
                load(d["qscratch"][1], qbl.rearrange("p m b h q -> p m (b h q)"), "q_out")
                sp.wait_ge(sem("q_out"), 32 * (layer + 1))
                for row, part in ((0, 0), (32, 0), (64, 1)):
                    for mt in range(2):
                        load(qs[row:row + 32, 4 * mt:4 * mt + 4, :, :].rearrange("r j b q -> r j (b q)"),
                             d["qscratch"][part][:, mt, :].rearrange("(j r) c -> r j c", j=4), "qs_in")
                restack(g0, 0, (1,))
                if layer == 0:
                    store_parts(0, 0)
                    load_ctx(2, 2)
                    store_parts(1, 1)

                def body(b, u):
                    g = g0 + b
                    ahead = isinstance(b, int) and b >= B - 3
                    lastb = isinstance(b, int) and b == B - 1
                    if not lastb:
                        restack(g + 1, 1 - u, (0,))
                    if layer == 1 and kind_of(b) in ("first", "inner"):
                        load_parts(g + 2, b + 2, u)
                    elif layer == 0 and kind_of(b) in ("next_to_last", "last"):
                        for u_ in range(2):
                            sp.wait_ge(sem(f"parts_stored{u_}"), 32 * ((b + 2 - u_) // 2))
                        load_parts(g + 2, b + 2 - B, u)
                    if not lastb:
                        restack(g + 1, 1 - u, (1,))
                    if layer == 0 and not ahead:
                        load_ctx(g + 3, b + 3)
                    if layer == 0 and kind_of(b) in ("first", "inner"):
                        store_parts(g + 2, u)

                each_batch(sp, layer, body)

                if layer == 0:
                    sp.wait_ge(sem("a_v"), 1)
                    for b in range(B):
                        load(d["scratch"][b].rearrange("h s c -> s h c"),
                             a_v[NQ * (b % 2):NQ * (b % 2) + NQ, b // 2, :].rearrange("s (h c) -> s h c", h=H),
                             "scratch_out")
                    sp.wait_ge(sem("scratch_out"), 16 * B)
                    load(a_w[:, :, :], d["scratch"].rearrange("b h (q s) c -> (b h q) (s c)", q=4)
                         .rearrange("(t p) c -> p t c", p=P), "a_w_in")
            sp.wait_ge(sem("moe_free"), 3)
            for h in range(2):
                sp.wait_ge(sem(f"parts_in{h}"), 32 * B)
            load(rw[:, :, :, :], d["rw"], "rw_in")
            load(rdw[:, :, :], d["rdw"], "rw_in")
            for w in range(2 * IT):
                if w >= 3:
                    sp.wait_ge(sem("wlo_done"), w - 2)
                load(w32[:, w % 3, :], d["wgu"][w], f"w_in{w % 3}")
            for e in range(E):
                w = 2 * IT + e
                sp.wait_ge(sem("wlo_done"), w - 2)
                load(w32[:, w % 3, :], d["wd"][e], f"w_in{w % 3}")
            sp.wait_ge(sem("x_final"), 1)
            load(out, x[:, :, :], "out_done")
            sp.wait_ge(sem("out_done"), 16)

        @block.gpsimd
        def _(pool):
            def load(dst, src, name):
                pool.dma_start(dst, src).then_inc(sem(name), 16)

            powers = [0]

            def inverse_root(tag):
                powers[0] += 1
                pool.wait_ge(sem("var_ready"), powers[0])
                nc.gpsimd.tensor_tensor(lnb[tag]["rstd"][:, :], lnb[tag]["ve"][:, :], half[:, :], ALU.pow)\
                  .then_inc(sem("rstd_ready"), 1)

            nc.gpsimd.memset(half[:, :], -0.5).then_inc(sem("half_ready"), 1)
            load(small[:, :], d["small"], "const_in")
            load(bias[:, :, :], d["bias"], "const_in")
            load(rows[:, :, :], d["rows"], "const_in")
            load(am[:, 0, :, :], d["am"], "am_in")
            load(wq[:, :, :], d["wq"][0], "wq_in")
            load(wo[:, :, :], d["wo"][0], "wo_in")

            def cross(layer):
                g0 = B * layer
                nc.gpsimd.memset(v[:, :, :, 32:33], 1.0).then_inc(sem("v_ones"), 1)

                def klo(g, units):
                    for ku in units:
                        mt, (k0, w) = ku // 4, QUARTERS[ku % 4]
                        pool.wait_ge(sem("khi_done"), K_UNITS * g + ku + 1)
                        need(pool, "klo_done", K_UNITS * g + ku)
                        nc.gpsimd.tensor_tensor(kl[:, mt, k0:k0 + w], k32[:, ku % 4, 0:w], kh[:, mt, k0:k0 + w],
                                                ALU.subtract).then_inc(sem("klo_done"), 1)

                klo(g0, range(8))
                klo(g0 + 1, range(4))

                def body(b, u):
                    g = g0 + b
                    for k in range(KT):
                        n, buf = TILE_ROWS[k], prob_buffer(u, k)
                        pool.wait_ge(sem("phi_done"), KT * g + k + 1)
                        nc.gpsimd.tensor_tensor(pl[0:n, buf, :], p32[0:n, exp_buffer(u, k), :], ph[0:n, buf, :],
                                                ALU.subtract).then_inc(sem("plo_done"), 1)
                        for name in STEP_UNITS[k]:
                            if name[0] in "KN"[layer:] and has_unit(kind_of(b), name):
                                klo(g + batches_ahead("inner", name), [int(name[1])])

                each_batch(pool, layer, body)

            pool.wait_ge(sem("half_ready"), 1)
            inverse_root("mid")
            cross(0)
            pool.wait_ge(sem("x_cross"), 1)
            pool.wait_ge(sem("mid_free"), 1)
            load(aw[:, :, :, :], d["aw"], "aw_in")
            load(fw32[:, :, :], d["fw"], "fw_in")
            load(fb32[:, :], d["fb"], "fw_in")
            load(wg[:, :, :], d["wg"], "wg_in")
            nc.gpsimd.memset(ones16[:, :], 1.0).then_inc(sem("ones16"), 1)
            load(wq[:, :, :], d["wq"][1], "wq_in")
            load(wo[:, :, :], d["wo"][1], "wo_in")
            load(wkv32[:, :, :, :], d["wkv"][1], "wkv1_in")
            for _ in range(3):
                inverse_root("mid")
            pool.wait_ge(sem("mid_done"), 3)
            cross(1)
            pool.wait_ge(sem("x_cross"), 2)
            load(bT[:, :, :], d["bT"], "ssm_in")
            load(cT[:, :], d["cT"], "ssm_in")
            inverse_root("ssm")
            inverse_root("ssm")
            inverse_root("moe")
            for it in range(IT):
                pool.wait_ge(sem("ihi_done"), it + 1)
                nc.gpsimd.tensor_tensor(il[:, it, :], i32[:, it % 2, :], ih[:, it, :],
                                        ALU.subtract).then_inc(sem("ilo_done"), 1)

        @block.tensor
        def _(pe):
            def mm(o, lhsT, rhs, start, stop, shared=False):
                return nc.tensor.matmul(o, lhsT, rhs, start=start, stop=stop, skip_group_check=shared)

            def use_slot(kind, g, name):
                before = last_use(kind, g, name)
                if before:
                    need(pe, *before)
                return slot[place(name, kind)]

            def input_ready(layer, g, h):
                if layer == 0:
                    pe.wait_ge(sem("clo_done"), 4 * g + 2 * h + 2)
                else:
                    for h_ in range(h + 1):
                        pe.wait_ge(sem(f"parts_in{h_}"), 32 * (g - B + 1))

            def k_unit(layer, g, u, ku, o):
                mt, (k0, w) = ku // 4, QUARTERS[ku % 4]
                input_ready(layer, g, ku % 4 // 2)
                for kc in range(KC):
                    for n, (a, c) in enumerate(((wkh, ch), (wkh, cl), (wkl, ch))):
                        last = mm(o[:, 0:w], a[layer][:, kc, mt * P:mt * P + P], c[u][:, kc, k0:k0 + w],
                                  kc == 0 and n == 0, kc == KC - 1 and n == 2)
                last.then_inc(sem("k_mm"), 1)

            def v_unit(layer, g, u, vu, o):
                input_ready(layer, g, int(P * (V_TILES[vu][-1] + 1) > HALF))
                for i, kt in enumerate(V_TILES[vu]):
                    n = TILE_ROWS[kt]
                    for kc in range(KC):
                        for m, (c, w) in enumerate(((ch, wvh), (ch, wvl), (cl, wvh))):
                            last = mm(o[0:n, D * i:D * i + D], c[u][:, kc, P * kt:P * kt + n], w[layer][:, kc, :],
                                      kc == 0 and m == 0, kc == KC - 1 and m == 2)
                last.then_inc(sem("v_mm"), 1)

            def p_unit(g, i, o):
                j, h = pair_and_half(i)
                k0, w = HALVES[h]
                r, mt = slice(32 * (j % 4), 32 * (j % 4) + 32), j // 4
                if i == 0:
                    pe.wait_ge(sem("qbcur_ready"), g + 1)
                pe.wait_ge(sem("khi_done"), K_UNITS * g + 4 * mt + 2 * h + 2)
                for a0, a1 in ((0, BANK), (BANK, w)):
                    last = mm(o[:, a0:a1], qbcur[r, mt, :], kh[r, mt, k0 + a0:k0 + a1], True, True)
                last.then_inc(sem("p_mm"), 1)

            def t_unit(g, o):
                pe.wait_ge(sem("m_ready"), g + 1)
                for j in range(NP):
                    last = mm(o[0:1, P * j:P * j + P], m16[:, j:j + 1], ident16[:, :], True, True)
                last.then_inc(sem("t_mm"), 1)

            def o_unit(g, o):
                pe.wait_ge(sem("o_norm"), g + 1)
                nc.tensor.transpose(o[:, 0:P], osum[:, :, :, :].rearrange("p b j d -> p (b j d)"),
                                    ident[:, :]).then_inc(sem("o_mm"), 1)

            def run_unit(layer, kind, g, u, name):
                letter, i = name[0], int(name[1:] or 0)
                o = use_slot(kind, g, name)
                ahead = batches_ahead(kind, name)
                gu, uu = g + ahead, (u, 1 - u)[ahead % 2]
                if letter in "KN":
                    k_unit(layer, gu, uu, i, o)
                elif letter == "V":
                    v_unit(layer, gu, uu, i, o)
                elif letter == "P":
                    p_unit(gu, i, o)
                elif letter == "T":
                    t_unit(gu, o)
                else:
                    o_unit(gu, o)

            def scores(g, u, k):
                n = TILE_ROWS[k]
                if k == 0:
                    pe.wait_ge(sem("qcur_ready"), g + 1)
                    pe.wait_ge(sem("row_done"), g + 1)
                    for mt in range(2):
                        pe.wait_ge(sem(f"stacked{mt}"), 16 * 12 * (g + 1))
                for hb in range(2):
                    need(pe, "exp_done", 2 * KT * g + 2 * k - 1 + hb)
                    for jj in range(4):
                        j = 4 * hb + jj
                        last = mm(ps[0:n, hb, P * jj:P * jj + P], ks[u][:, j, P * k:P * k + n], qcur[u][:, j, :],
                                  True, True)
                    last.then_inc(sem("main_mm"), 1)

            def weigh(g, u, k):
                n, buf = TILE_ROWS[k], prob_buffer(u, k)
                if k == 0:
                    need(pe, "o_norm", g)
                if k % 2 == 0:
                    pe.wait_ge(sem("vlo_done"), V_UNITS * g + k // 2 + 1)
                pe.wait_ge(sem("plo_done"), KT * g + k + 1)
                for j in range(NP):
                    o = pvb[:, j // 4, j % 4, :]
                    mm(o[:, :], ph[0:n, buf, P * j:P * j + P], v[0:n, k, j, :], k == 0 and j % 4 == 0, k == KT - 1, True)
                    last = mm(o[:, 0:33], pl[0:n, buf, P * j:P * j + P], v[0:n, k, j, 0:33], False, k == KT - 1, True)
                last.then_inc(sem("pv_mm"), 1)

            def cross(layer):
                g0 = B * layer
                pe.wait_ge(sem("kvw_ready"), layer + 1)
                for name in PROLOGUE_UNITS:
                    if name == "Q":
                        transposes(3 * layer, "mid", 6)
                        pe.wait_ge(sem("wq_in"), 16 * (layer + 1))
                        q_projection(layer)
                        continue
                    run_unit(layer, "prologue", g0, 0, name)
                pe.wait_ge(sem("ones_in"), 32 * (layer + 1))

                def body(b, u):
                    g, kind = g0 + b, kind_of(b)
                    for k in range(KT):
                        for name in STEP_UNITS[k]:
                            if not has_unit(kind, name):
                                continue
                            if name == "S":
                                scores(g, u, k)
                            elif name == "W" and k >= LAG:
                                weigh(g, u, k - LAG)
                            elif name == "W":
                                if kind != "first":
                                    weigh(g - 1, 1 - u, KT + k - LAG)
                            else:
                                run_unit(layer, kind, g, u, name)
                    if kind == "last":
                        for k in range(KT - LAG, KT):
                            weigh(g, u, k)
                        run_unit(layer, "end", g, u, "O")

                each_batch(pe, layer, body)

            def transposes(m, tag, bank=4):
                for t in range(TT):
                    pe.wait_ge(sem("xn_ready"), TT * m + t + 1)
                    for kc in range(KC):
                        last = nc.tensor.transpose(ps[:, bank + kc, P * t:P * t + P], lnb[tag]["xn"][:, t, P * kc:P * kc + P],
                                                   ident[:, :])
                last.then_inc(sem("xnT_mm"), 1)
                pe.wait_ge(sem("xnT_ready"), m + 1)

            def q_projection(layer):
                for mt in range(2):
                    for kc in range(KC):
                        last = mm(ps[:, mt, :], wq[:, kc, P * mt:P * mt + P], lnb["mid"]["xnT"][:, kc, :],
                                  kc == 0, kc == KC - 1)
                last.then_inc(sem("q_mm"), 1)

            def out_projection(layer):
                pe.wait_ge(sem("oT_done"), B * (layer + 1))
                pe.wait_ge(sem("wo_in"), 16 * (layer + 1))
                for t in range(TT):
                    for e in range(2):
                        last = mm(ps[:, t // 2, D * (t % 2):D * (t % 2) + D], oT[:, e, P * t:P * t + P], wo[:, e, :],
                                  e == 0, e == 1)
                last.then_inc(sem("xo_mm"), 1)

            pe.wait_ge(sem("ident_in"), 16)
            pe.wait_ge(sem("const_ready"), 1)
            cross(0)
            out_projection(0)

            transposes(1, "mid")
            xnT = lnb["mid"]["xnT"]
            pe.wait_ge(sem("aw_in"), 16)
            pe.wait_ge(sem("x_cross"), 1)
            for t in range(TT):
                for kc in range(KC):
                    last = mm(ps[:, 6 + t // 2, D * (t % 2):D * (t % 2) + D], xnT[:, kc, P * t:P * t + P],
                              aw[:, 2, kc, :], kc == 0, kc == KC - 1)
            last.then_inc(sem("a_v_mm"), 1)
            for t in range(TT):
                for kc in range(KC):
                    last = mm(ps[:, t, :].rearrange("p (w c) -> p w c", w=2), xnT[:, kc, P * t:P * t + P],
                              aw[:, 0:2, kc, :], kc == 0, kc == KC - 1)
                last.then_inc(sem("a_qk_mm"), 1)
            pe.wait_ge(sem("a_qk"), TT)
            for t in range(TT):
                for r in (slice(0, 64), slice(64, 128)):
                    for c in range(DH):
                        last = mm(ps[r, 4, H * t:H * t + H], a_q[r, t, c, :, :].rearrange("p a f -> p (a f)"),
                                  a_k[r, t, c:D:DH], c == 0, c == DH - 1)
            last.then_inc(sem("a_e_mm"), 1)
            pe.wait_ge(sem("a_w_in"), 16)
            pe.wait_ge(sem("a_v"), 1)
            for t in range(TT):
                for kc in range(KC):
                    last = nc.tensor.transpose(ps[:, 6 + kc, P * t:P * t + P], a_w[:, t, P * kc:P * kc + P],
                                               ident[:, :])
            last.then_inc(sem("a_wT_mm"), 1)
            pe.wait_ge(sem("a_wT"), 1)
            for t in range(TT):
                for kc in range(KC):
                    last = mm(ps[:, t // 2, D * (t % 2):D * (t % 2) + D], a_wT[:, kc, P * t:P * t + P],
                              aw[:, 3, kc, :], kc == 0, kc == KC - 1)
            last.then_inc(sem("a_z_mm"), 1)
            pe.wait_ge(sem("a_mT"), 1)
            for t in range(TT):
                last = nc.tensor.transpose(ps[:, 5, P * t:P * t + P], a_mT[:, t, :], ident[:, :])
            last.then_inc(sem("a_m_mm"), 1)
            pe.wait_ge(sem("a_m_ready"), 1)
            pe.wait_ge(sem("a_z"), 1)
            for t in range(TT):
                last = mm(ps[:, 2 + t // 2, D * (t % 2):D * (t % 2) + D], a_m[:, t, :], a_z[:, t, :], True, True)
            last.then_inc(sem("a_x_mm"), 1)

            transposes(2, "mid")
            f = lnb["mid"]
            pe.wait_ge(sem("wg_in"), 16)
            for t in range(TT):
                for kc in range(KC):
                    last = mm(ps[:, t // 2, D * (t % 2):D * (t % 2) + D], f["xnT"][:, kc, P * t:P * t + P],
                              wg[:, kc, :], kc == 0, kc == KC - 1)
            last.then_inc(sem("f_l_mm"), 1)
            pe.wait_ge(sem("fw_ready"), 2)
            pe.wait_ge(sem("xl_ready"), 1)
            pe.wait_ge(sem("ones16"), 1)
            for i in range(TT * E // 2):
                t, c = i // 4, slice(2 * D * (i % 4), 2 * D * (i % 4) + 2 * D)
                if i >= 4:
                    pe.wait_ge(sem("f_r"), 2 * (i - 3))
                o = ps[:, 4 + i % 4, :]
                if i == 0:
                    pe.wait_ge(sem("x_attn"), 1)
                mm(o, ones16[:, :], fbh[:, c], True, False)
                mm(o, ones16[:, :], fbl[:, c], False, False)
                for kc in range(KC):
                    for n, (a, w) in enumerate(((f["h"], fwh), (f["h"], fwl), (f["l"], fwh))):
                        last = mm(o, a[:, kc, P * t:P * t + P], w[:, kc, c], False, kc == KC - 1 and n == 2)
                last.then_inc(sem("f_mm"), 1)
            pe.wait_ge(sem("mid_done"), 3)
            cross(1)
            out_projection(1)

            transposes(4, "ssm")
            xnT = lnb["ssm"]["xnT"]
            pe.wait_ge(sem("ssm_in"), 32)
            for kc in range(KC):
                last = mm(ps[0:N, 2, :], bT[:, kc, :], xnT[:, kc, :], kc == 0, kc == KC - 1)
            last.then_inc(sem("u_mm"), 1)
            pe.wait_ge(sem("am_in"), 16)
            for k in range(6):
                back = 1 << k
                pe.wait_ge(sem("scan"), k + 1)
                if k > 0:
                    pe.wait_ge(sem("am_pow"), k)
                mm(ps[0:N, 3, 0:B * (NQ - back)], am[:, k, 1, :], st_s[:, :, 0:NQ - back], True,
                   True).then_inc(sem("scan_mm"), 1)
                if k < 5:
                    mm(ps[0:N, 0, 0:N], am[:, k, 1, :], am[:, k, 0, :], True, True)
                    mm(ps[0:N, 1, 0:N], am[:, k, 0, :], am[:, k, 1, :], True, True).then_inc(sem("am_mm"), 1)
            pe.wait_ge(sem("scan"), 7)
            for t in range(TT):
                last = mm(ps[:, 6 + t // 2, D * (t % 2):D * (t % 2) + D],
                          st_s[:, 2 * t:2 * t + 2, :].rearrange("n b q -> n (b q)"), cT[:, :], True, True)
            last.then_inc(sem("y_mm"), 1)

            transposes(5, "moe")
            xnT = lnb["moe"]["xnT"]
            pe.wait_ge(sem("rw_in"), 32)
            for t in range(TT):
                for kc in range(KC):
                    last = mm(ps[:, 6, 2 * E * t:2 * E * t + 2 * E], xnT[:, kc, P * t:P * t + P],
                              rw[:, kc, :, :].rearrange("p r e -> p (r e)"), kc == 0, kc == KC - 1)
            last.then_inc(sem("r_mm"), 1)

            def scaled_transposes(i):
                pe.wait_ge(sem(f"xc_ready{i % 2}"), i // 2 + 1)
                if i >= 2:
                    pe.wait_ge(sem("xcl_ready"), i - 1)
                for t in range(TT):
                    for kc in range(KC):
                        last = nc.tensor.transpose(ps[:, 4 + 2 * (i % 2) + kc, P * t:P * t + P],
                                                   xc[:, i % 2, t, P * kc:P * kc + P], ident[:, :])
                last.then_inc(sem("xcT_mm"), 1)

            def router_down(it):
                pe.wait_ge(sem("inter"), it + 1)
                last = mm(ps[0:E, 4, :], rdw[:, it, :], i32[:, it % 2, :], it == 0, it == IT - 1)
                last.then_inc(sem("rd_mm"), 1)

            scaled_transposes(0)
            scaled_transposes(1)
            for w in range(2 * IT):
                it, r = w // 2, w % 2
                bank = 2 * (it % 2) + r
                if it >= 2:
                    pe.wait_ge(sem("inter"), it - 1)
                pe.wait_ge(sem("wlo_done"), w + 1)
                for e in range(E):
                    if it == 0:
                        pe.wait_ge(sem("xcl_ready"), E * r + e + 1)
                        if E * r + e + 2 < 2 * E:
                            scaled_transposes(E * r + e + 2)
                    for kc in range(KC):
                        c = (kc * E + e) * P
                        for n, (a, b_) in enumerate(((wh, xch), (wh, xcl), (wl, xch))):
                            last = mm(ps[:, bank, :], a[:, w % 2, c:c + P], b_[r][:, e, kc, :],
                                      e == 0 and kc == 0 and n == 0, e == E - 1 and kc == KC - 1 and n == 2)
                last.then_inc(sem("gu_mm"), 1)
                if r == 1 and it >= 1:
                    router_down(it - 1)
            router_down(IT - 1)
            pe.wait_ge(sem("ldT_ready"), 1)
            for t in range(TT):
                last = nc.tensor.transpose(ps[:, 5, E * t:E * t + E], ldT[:, P * t:P * t + P], ident[0:E, 0:E])
            last.then_inc(sem("ld_mm"), 1)
            for e in range(E):
                w = 2 * IT + e
                pe.wait_ge(sem("wlo_done"), w + 1)
                if e == 0:
                    pe.wait_ge(sem("ilo_done"), IT)
                    pe.wait_ge(sem("inter"), IT)
                if e >= 2:
                    pe.wait_ge(sem("y_added"), e - 1)
                for t in range(TT):
                    o = ps[:, 2 * (e % 2) + t // 2, D * (t % 2):D * (t % 2) + D]
                    for it in range(IT):
                        c = slice(D * it, D * it + D)
                        for n, (a, b_) in enumerate(((ih, wh), (ih, wl), (il, wh))):
                            last = mm(o, a[:, it, P * t:P * t + P], b_[:, w % 2, c], it == 0 and n == 0,
                                      it == IT - 1 and n == 2)
                last.then_inc(sem("d_mm"), 1)

        @block.scalar
        def _(act):
            def copy_T(m, tag, parts=False, bank=4):
                act.wait_ge(sem("xnT_mm"), m + 1)
                nc.scalar.activation(lnb[tag]["xnT"][:, :, :], ps[:, bank:bank + 2, :], ACT.Copy)\
                   .then_inc(sem("xnT_ready"), 1)
                if parts:
                    act.wait_ge(sem("xnT_ready"), m + 1)
                    nc.scalar.activation(lnb[tag]["h"][:, :, :], lnb[tag]["xnT"][:, :, :], ACT.Copy)\
                       .then_inc(sem("xh_ready"), 1)

            def split_kv(layer):
                act.wait_ge(sem(f"wkv{layer}_in"), 16)
                nc.scalar.activation(wkh[layer][:, :, :], wkv32[:, :, 0, :], ACT.Copy, scale=W_SCALE)
                nc.scalar.activation(wvh[layer][:, :, :], wkv32[:, :, 1, :], ACT.Copy, scale=W_SCALE)\
                   .then_inc(sem("kvh_ready"), 1)

            def split_ctx(g, u, i):
                h, kc = i // 2, i % 2
                k0, w = HALVES[h]
                act.wait_ge(sem(f"ctx_in{h}"), 16 * (g + 1))
                need(act, "v_mm", V_UNITS * (g - 2) + (4 if h == 0 else V_UNITS))
                need(act, f"parts_stored{u}", 16 * g - 16 * u)
                nc.scalar.activation(ch[u][:, kc, k0:k0 + w], c32[:, h, kc, 0:w], ACT.Copy).then_inc(sem("chi_done"), 1)

            def after_unit(layer, kind, g, b, u, name):
                letter, i = name[0], int(name[1:] or 0)
                o = slot[place(name, kind)]
                ahead = batches_ahead(kind, name)
                gu = g + ahead
                if letter in "KN":
                    mt, (k0, w) = i // 4, QUARTERS[i % 4]
                    act.wait_ge(sem("k_mm"), K_UNITS * gu + i + 1)
                    need(act, "klo_done", K_UNITS * gu + i - 3)
                    need(act, f"stacked{mt}", 16 * 12 * gu)
                    how = dict(scale=1 / W_SCALE)
                    func = ACT.Copy
                    if layer:
                        func, how["bias"] = ACT.Identity, bias[:, 1, mt:mt + 1]
                    nc.scalar.activation(k32[:, i % 4, 0:w], o[:, 0:w], func, **how).then_inc(sem("k32_done"), 1)
                    nc.scalar.activation(kh[:, mt, k0:k0 + w], o[:, 0:w], func, **how).then_inc(sem("khi_done"), 1)
                elif letter == "V":
                    kts = V_TILES[i]
                    n = TILE_ROWS[kts[0]]
                    act.wait_ge(sem("v_mm"), V_UNITS * gu + i + 1)
                    need(act, "pv_mm", KT * (gu - 1) + kts[-1] + 1)
                    nc.scalar.activation(v[0:n, kts[0]:kts[-1] + 1, :, 0:32],
                                         o[0:n, 0:D * len(kts)].rearrange("p (k j c) -> p k j c", j=NP, c=32),
                                         ACT.Copy, scale=1 / W_SCALE).then_inc(sem("vhi_done"), 1)
                elif letter == "T":
                    uu = (u, 1 - u)[ahead]
                    act.wait_ge(sem("t_mm"), gu + 1)
                    need(act, "main_mm", 2 * KT * (gu - 1))
                    nc.scalar.activation(qcur[uu][STACK:STACK + 1, :, :],
                                         o[0:1, :].rearrange("p (j q) -> p j q", j=NP), ACT.Copy, scale=-1.0)\
                       .then_inc(sem("row_done"), 1)
                elif letter == "O":
                    bo = b + ahead
                    act.wait_ge(sem("o_mm"), gu + 1)
                    for e in range(2):
                        dst, src = oT[:, e, bass.ds(NQ * bo, NQ)], o[:, NQ * e:NQ * e + NQ]
                        if layer:
                            ins = nc.scalar.activation(dst, src, ACT.Identity, bias=bias[:, 2, e:e + 1])
                        else:
                            ins = nc.scalar.activation(dst, src, ACT.Copy)
                    ins.then_inc(sem("oT_done"), 1)

            def exps(g, u, k):
                n = TILE_ROWS[k]
                need(act, "plo_done", KT * g + k - steps_back(exp_buffer, u, k) + 1)
                for hb in range(2):
                    act.wait_ge(sem("main_mm"), 2 * KT * g + 2 * k + hb + 1)
                    nc.scalar.activation(p32[0:n, exp_buffer(u, k), BANK * hb:BANK * hb + BANK], ps[0:n, hb, :],
                                         ACT.Exp, scale=DH ** -0.5).then_inc(sem("exp_done"), 1)

            def cross(layer):
                g0 = B * layer
                if layer == 0:
                    for i in range(4):
                        split_ctx(0, 0, i)
                for name in PROLOGUE_UNITS:
                    if name == "Q":
                        copy_T(3 * layer, "mid", bank=6)
                        if layer == 0:
                            for i in range(4):
                                split_ctx(1, 1, i)
                        act.wait_ge(sem("q_mm"), layer + 1)
                        for mt in range(2):
                            if layer:
                                ins = nc.scalar.activation(q32[:, mt, :], ps[:, mt, :], ACT.Identity,
                                                           bias=bias[:, 0, mt:mt + 1])
                            else:
                                ins = nc.scalar.activation(q32[:, mt, :], ps[:, mt, :], ACT.Copy)
                            ins.then_inc(sem("q32_done"), 1)
                        continue
                    after_unit(layer, "prologue", g0, 0, 0, name)

                def body(b, u):
                    g, kind = g0 + b, kind_of(b)
                    for k in range(KT):
                        for name in STEP_UNITS[k]:
                            if name == "S":
                                exps(g, u, k)
                            elif name != "W" and has_unit(kind, name):
                                after_unit(layer, kind, g, b, u, name)
                        if k in CTX_STEPS and layer == 0 and kind in ("first", "inner"):
                            split_ctx(g + 2, u, CTX_STEPS[k])
                    if kind == "last":
                        after_unit(layer, "end", g, b, u, "O")

                each_batch(act, layer, body)

            act.dma_start(ident[:, :], d["ident"]).then_inc(sem("ident_in"), 16)
            split_kv(0)
            cross(0)

            act.wait_ge(sem("mid_free"), 1)
            copy_T(1, "mid")
            for t in range(2):
                act.wait_ge(sem("a_qk_mm"), t + 1)
                nc.scalar.activation(a_q[:, t, :, :, :], heads_by_dim(ps[:, t, 0:D]), ACT.Copy)
                nc.scalar.activation(a_k[:, t, :], ps[:, t, D:2 * D], ACT.Copy).then_inc(sem("a_qk"), 1)
            act.wait_ge(sem("fw_in"), 32)
            nc.scalar.activation(fwh[:, :, :], fw32[:, :, :], ACT.Copy, scale=W_SCALE)
            nc.scalar.activation(fbh[:, :], fb32[:, :], ACT.Copy, scale=W_SCALE).then_inc(sem("fwh_ready"), 1)
            act.wait_ge(sem("a_max"), 1)
            for t in range(TT):
                ins = nc.scalar.activation(a_e[:, t, :], ps[:, 4, H * t:H * t + H], ACT.Exp, scale=DH ** -0.5,
                                           bias=a_s[:, 1, t:t + 1], accum_out=a_s[:, 2, t:t + 1])
            ins.then_inc(sem("a_exp"), 1)
            act.wait_ge(sem("a_wT_mm"), 1)
            nc.scalar.activation(a_wT[:, :, :], ps[:, 6:8, :], ACT.Copy).then_inc(sem("a_wT"), 1)
            act.wait_ge(sem("a_m_mm"), 1)
            nc.scalar.activation(a_m[:, :, :], ps[:, 5, :].rearrange("p (t c) -> p t c", t=TT), ACT.Copy)\
               .then_inc(sem("a_m_ready"), 1)

            copy_T(2, "mid", parts=True)
            act.wait_ge(sem("f_m"), 1)
            for t in range(TT):
                ins = nc.scalar.activation(ex[:, t, :], lg[:, t, :], ACT.Exp, bias=f_s[:, 0, t:t + 1],
                                           accum_out=f_s[:, 1, t:t + 1])
            ins.then_inc(sem("f_e"), 1)
            act.wait_ge(sem("f_w"), 1)
            for i in range(TT * E // 2):
                act.wait_ge(sem("f_mm"), i + 1)
                for n in range(2):
                    q = 2 * i + n
                    e = 2 * (i % 4) + n
                    if q >= 4:
                        act.wait_ge(sem("f_add"), q - 3)
                    nc.scalar.activation(f_y[:, q % 4, :], ps[:, 4 + i % 4, D * n:D * n + D], ACT.Relu,
                                         scale=f_w[:, i // 4, e:e + 1]).then_inc(sem("f_r"), 1)
            split_kv(1)
            nc.scalar.nop().then_inc(sem("mid_done"), 1)

            act.wait_ge(sem("mid_done"), 3)
            act.wait_ge(sem("const_in"), 48)
            cross(1)

            copy_T(4, "ssm")
            act.wait_ge(sem("u_mm"), 1)
            nc.scalar.activation(st_s[:, :, :], ps[0:N, 2, :].rearrange("n (b q) -> n b q", b=B), ACT.Copy)\
               .then_inc(sem("scan"), 1)
            for k in range(1, 6):
                act.wait_ge(sem("am_mm"), k)
                nc.scalar.activation(am[:, k, :, :], ps[0:N, 0:2, 0:N], ACT.Copy).then_inc(sem("am_pow"), 1)
            act.wait_ge(sem("y_mm"), 1)
            nc.scalar.activation(g_a[:, :, :], ps[:, 6:8, :].rearrange("p b (t c) -> p (b t) c", t=2), ACT.Gelu)\
               .then_inc(sem("gelu"), 1)

            nc.scalar.nop().then_inc(sem("moe_free"), 1)
            act.wait_ge(sem("moe_free"), 3)
            for h in range(2):
                act.wait_ge(sem(f"parts_in{h}"), 32 * B)
            copy_T(5, "moe")

            def split_w(w):
                act.wait_ge(sem(f"w_in{w % 3}"), 16 * (w // 3 + 1))
                if w == 2 * IT or w == 2 * IT + 1:
                    act.wait_ge(sem("gu_mm"), w - 1)
                elif w > 2 * IT:
                    act.wait_ge(sem("d_mm"), w - 2 * IT - 1)
                elif w >= 2:
                    act.wait_ge(sem("gu_mm"), w - 1)
                nc.scalar.activation(wh[:, w % 2, :], w32[:, w % 3, :], ACT.Copy, scale=W_SCALE)\
                   .then_inc(sem("whi_done"), 1)

            def exp_gap(n):
                act.wait_ge(sem("r_top"), n + 1)
                lo, hi = (0, 2 * TT) if n == 0 else (2 * TT, 3 * TT)
                nc.scalar.activation(pr[:, lo:hi, 1:2], prt[:, lo:hi, 1:2], ACT.Exp).then_inc(sem("r_exp"), 1)

            def inner(it):
                act.wait_ge(sem("gu_mm"), 2 * it + 1)
                need(act, "inter", it)
                nc.scalar.activation(sg[:, 0, :], ps[:, 2 * (it % 2), :], ACT.Exp, scale=-1 / W_SCALE)\
                   .then_inc(sem("sg"), 1)
                act.wait_ge(sem("inter"), it + 1)
                nc.scalar.activation(ih[:, it, :], i32[:, it % 2, :], ACT.Copy).then_inc(sem("ihi_done"), 1)

            split_w(0)
            split_w(1)
            exp_gap(0)

            def scale_tokens(i):
                r, e = i // E, i % E
                for t in range(TT):
                    ins = nc.scalar.activation(xc[:, 1, t, :], lnb["moe"]["xn"][:, t, :], ACT.Copy,
                                               scale=cmb[:, TT * r + t, e:e + 1])
                ins.then_inc(sem("xc_ready1"), 1)

            act.wait_ge(sem("cmb_ready"), 1)
            scale_tokens(1)
            for i in range(2 * E):
                act.wait_ge(sem("xcT_mm"), i + 1)
                b_ = 4 + 2 * (i % 2)
                nc.scalar.activation(xch[i // E][:, i % E, :, :], ps[:, b_:b_ + 2, :], ACT.Copy)\
                   .then_inc(sem("xch_ready"), 1)
                if i % 2 == 1 and i + 2 < 2 * E:
                    scale_tokens(i + 2)
                if i == E:
                    split_w(2)
            for w in range(3, 2 * IT):
                split_w(w)
                if w % 2 == 1:
                    inner(w // 2 - 1)
            split_w(2 * IT)
            inner(IT - 1)
            act.wait_ge(sem("rd_mm"), IT)
            nc.scalar.activation(ldT[:, :], ps[0:E, 4, :], ACT.Copy).then_inc(sem("ldT_ready"), 1)
            split_w(2 * IT + 1)
            exp_gap(1)
            for e in range(2, E):
                split_w(2 * IT + e)

        @block.vector
        def _(dve):
            chained, powers = [0], [0]

            def link(ins):
                chained[0] += 1
                ins.then_inc(sem("dve_chain"), 1)
                dve.wait_ge(sem("dve_chain"), chained[0])

            def stats(tag, src):
                st, mv = lnb[tag]["st"], lnb[tag]["mv"]
                for t in range(TT):
                    ins = nc.vector.bn_stats(st[:, t, :], src[:, t, :])
                link(ins)
                for t in range(TT):
                    ins = nc.vector.bn_aggr(mv[:, t, :], st[:, t, :])
                link(ins)
                nc.vector.tensor_scalar(lnb[tag]["ve"][:, :].unsqueeze(2), mv[:, :, 1:2], LN_EPS, None, ALU.add)\
                  .then_inc(sem("var_ready"), 1)
                powers[0] += 1
                dve.wait_ge(sem("rstd_ready"), powers[0])

            def layernorm(tag, src, dst):
                stats(tag, src)
                mv, rstd = lnb[tag]["mv"], lnb[tag]["rstd"]
                for t in range(TT):
                    yield nc.vector.tensor_scalar(dst[:, t, :], src[:, t, :], mv[:, t, 0:1], rstd[:, t:t + 1],
                                                  ALU.subtract, ALU.mult)

            def norm_x(tag):
                for ins in layernorm(tag, x, lnb[tag]["xn"]):
                    ins.then_inc(sem("xn_ready"), 1)

            def split_kv(layer):
                dve.wait_ge(sem("kvh_ready"), layer + 1)
                for n, (hi, lo) in enumerate(((wkh, wkl), (wvh, wvl))):
                    ins = nc.vector.scalar_tensor_tensor(lo[layer][:, :, :], wkv32[:, :, n, :], W_SCALE,
                                                         hi[layer][:, :, :], ALU.mult, ALU.subtract)
                ins.then_inc(sem("kvw_ready"), 1)

            def split_ctx(g, u, i):
                h, kc = i // 2, i % 2
                k0, w = HALVES[h]
                dve.wait_ge(sem("chi_done"), 4 * g + i + 1)
                nc.vector.tensor_tensor(cl[u][:, kc, k0:k0 + w], c32[:, h, kc, 0:w], ch[u][:, kc, k0:k0 + w],
                                        ALU.subtract).then_inc(sem("clo_done"), 1)

            def after_unit(kind, g, name):
                letter, i = name[0], int(name[1:] or 0)
                o = slot[place(name, kind)]
                gu = g + batches_ahead(kind, name)
                if letter == "V":
                    kts = V_TILES[i]
                    n = TILE_ROWS[kts[0]]
                    dve.wait_ge(sem("vhi_done"), V_UNITS * gu + i + 1)
                    nc.vector.scalar_tensor_tensor(
                        v[0:n, kts[0]:kts[-1] + 1, :, 33:65],
                        o[0:n, 0:D * len(kts)].rearrange("p (k j c) -> p k j c", j=NP, c=32), 1 / W_SCALE,
                        v[0:n, kts[0]:kts[-1] + 1, :, 0:32], ALU.mult, ALU.subtract).then_inc(sem("vlo_done"), 1)
                elif letter == "K":
                    mt, (k0, w) = i // 4, QUARTERS[i % 4]
                    dve.wait_ge(sem("khi_done"), K_UNITS * gu + i + 1)
                    dve.wait_ge(sem("klo_done"), K_UNITS * gu + i)
                    nc.vector.tensor_tensor(kl[:, mt, k0:k0 + w], k32[:, i % 4, 0:w], kh[:, mt, k0:k0 + w],
                                            ALU.subtract).then_inc(sem("klo_done"), 1)
                elif letter == "P":
                    j, h = pair_and_half(i)
                    w = HALVES[h][1]
                    dve.wait_ge(sem("p_mm"), 2 * NP * gu + i + 1)
                    if i == 0:
                        need(dve, "m32_done", gu)
                    nc.vector.reduce_max(mpart[:, j, h:h + 1], o[:, 0:w], AX.X).then_inc(sem("max_done"), 1)
                elif letter == "T":
                    max_ready(gu)

            def max_ready(g):
                dve.wait_ge(sem("max_done"), 2 * NP * (g + 1))
                need(dve, "m_ready", g)
                nc.vector.tensor_tensor(m32[:, :].unsqueeze(2), mpart[:, :, 0:1], mpart[:, :, 1:2], ALU.max)\
                   .then_inc(sem("m32_done"), 1)
                dve.wait_ge(sem("m32_done"), g + 1)
                need(dve, "t_mm", g)
                nc.vector.tensor_scalar(m16[:, :], m32[:, :], 1 / M_SCALE, None, ALU.mult).then_inc(sem("m_ready"), 1)

            def take_high_queries(g, b):
                need(dve, "p_mm", 2 * NP * g)
                nc.vector.tensor_copy(qbcur[:, :, :].rearrange("p m (h q) -> p m h q", h=2), qbh[:, :, b, :, :])\
                  .then_inc(sem("qbcur_ready"), 1)

            def take_queries(g, b, u):
                need(dve, "main_mm", 2 * KT * (g - 1))
                nc.vector.tensor_copy(qcur[u][0:STACK, :, :], qs[:, :, b, :]).then_inc(sem("qcur_ready"), 1)

            def normalise(g):
                dve.wait_ge(sem("pv_mm"), KT * (g + 1))
                nc.vector.reciprocal(rinv[:, :, :].unsqueeze(3), pvb[:, :, :, 32:33])
                for r, c in ((slice(0, 64), 0), (slice(64, 128), DH)):
                    ins = nc.vector.tensor_copy(osum[r, :, :, :], pvb[r, :, :, c:c + DH])
                ins.then_inc(sem("o_step"), 1)
                dve.wait_ge(sem("o_step"), 2 * g + 1)
                for r, c in ((slice(0, 64), 33), (slice(64, 128), 33 + DH)):
                    ins = nc.vector.tensor_tensor(opart[r, :, :, :], osum[r, :, :, :], pvb[r, :, :, c:c + DH], ALU.add)
                ins.then_inc(sem("o_step"), 1)
                dve.wait_ge(sem("o_step"), 2 * g + 2)
                nc.vector.tensor_tensor(osum[:, :, :, :], opart[:, :, :, :],
                                        rinv[:, :, :].unsqueeze(3).broadcast_to([P, 2, 4, DH]), ALU.mult)\
                   .then_inc(sem("o_norm"), 1)

            def high_parts(g, u, k):
                n, buf = TILE_ROWS[k], prob_buffer(u, k)
                dve.wait_ge(sem("exp_done"), 2 * KT * g + 2 * k + 2)
                need(dve, "pv_mm", KT * g + k - steps_back(prob_buffer, u, k) + 1)
                nc.vector.tensor_copy(ph[0:n, buf, :], p32[0:n, exp_buffer(u, k), :]).then_inc(sem("phi_done"), 1)

            def cross(layer):
                g0 = B * layer
                if layer == 0:
                    for i in range(4):
                        split_ctx(0, 0, i)
                dve.wait_ge(sem("v_ones"), layer + 1)
                for name in PROLOGUE_UNITS:
                    if name == "Q":
                        dve.wait_ge(sem("q32_done"), 2 * (layer + 1))
                        link(nc.vector.tensor_copy(qh[:, :, :], q32[:, :, :]))
                        link(nc.vector.tensor_tensor(ql[:, :, :], q32[:, :, :], qh[:, :, :], ALU.subtract))
                        for dst, src in ((qbh, qh), (qbl, ql)):
                            for side in range(2):
                                ins = nc.vector.tensor_scalar(dst[:, :, :, side, :],
                                                              src[:, :, :].rearrange("p m (b q) -> p m b q", b=B),
                                                              small[:, SM_EVEN + side:SM_EVEN + side + 1], None, ALU.mult)
                        ins.then_inc(sem("qb_ready"), 1)
                        dve.wait_ge(sem("qb_ready"), layer + 1)
                        take_high_queries(g0, 0)
                        continue
                    if name == "T":
                        dve.wait_ge(sem("qs_in"), 16 * 6 * (layer + 1))
                        take_queries(g0, 0, 0)
                    if name[0] in "VPT":
                        after_unit("prologue", g0, name)
                    if name == "K3" and layer == 0:
                        for i in range(4):
                            split_ctx(1, 1, i)

                def body(b, u):
                    g, kind = g0 + b, kind_of(b)
                    for k in range(KT):
                        if k == 0 and kind != "last":
                            take_high_queries(g + 1, b + 1)
                        for name in STEP_UNITS[k]:
                            if name == "S":
                                if k > 0:
                                    high_parts(g, u, k - 1)
                                if k == LAG and kind != "first":
                                    normalise(g - 1)
                                for late in STEP_UNITS[k][:1] + STEP_UNITS.get(k - 1, [])[1:]:
                                    if late[0] in ("V", "VK"[layer]) and has_unit(kind, late):
                                        after_unit(kind, g, late)
                                if k == 1 and kind != "last":
                                    take_queries(g + 1, b + 1, 1 - u)
                            elif name[0] in "PTO" and has_unit(kind, name):
                                after_unit(kind, g, name)
                        if k == LAG + 4:
                            need(dve, "o_mm", g)
                        if k in CTX_STEPS and layer == 0 and kind in ("first", "inner"):
                            split_ctx(g + 2, u, CTX_STEPS[k])
                    high_parts(g, u, KT - 1)
                    if kind == "last":
                        normalise(g)

                each_batch(dve, layer, body)

                dve.wait_ge(sem("xo_mm"), layer + 1)
                o = ps[:, 0:2, :].rearrange("p b (t c) -> p (b t) c", t=2)
                link(nc.vector.tensor_tensor(x[:, :, :], x[:, :, :], o, ALU.add))
                if layer:
                    link(nc.vector.tensor_tensor(x[:, :, :], x[:, :, :],
                                                 rows[:, 2:3, :].broadcast_to([P, TT, D]), ALU.add))
                nc.vector.nop().then_inc(sem("x_cross"), 1)

            dve.wait_ge(sem("x_in"), 16)
            norm_x("mid")
            dve.wait_ge(sem("ident_in"), 16)
            nc.vector.tensor_copy(ident16[:, :], ident[:, :]).then_inc(sem("const_ready"), 1)
            split_kv(0)
            dve.wait_ge(sem("const_in"), 48)
            cross(0)

            dve.wait_ge(sem("plo_done"), KT * B)
            nc.vector.nop().then_inc(sem("mid_free"), 1)
            norm_x("mid")
            dve.wait_ge(sem("a_v_mm"), 1)
            nc.vector.tensor_copy(a_v[:, :, :], ps[:, 6:8, :].rearrange("p b (t c) -> p (b t) c", t=2))\
              .then_inc(sem("a_v"), 1)
            for t in range(2, TT):
                dve.wait_ge(sem("a_qk_mm"), t + 1)
                nc.vector.tensor_copy(a_q[:, t, :, :, :], heads_by_dim(ps[:, t, 0:D]))
                nc.vector.tensor_copy(a_k[:, t, :], ps[:, t, D:2 * D]).then_inc(sem("a_qk"), 1)
            dve.wait_ge(sem("fwh_ready"), 1)
            nc.vector.scalar_tensor_tensor(fwl[:, :, :], fw32[:, :, :], W_SCALE, fwh[:, :, :], ALU.mult,
                                           ALU.subtract).then_inc(sem("fw_ready"), 1)
            nc.vector.scalar_tensor_tensor(fbl[:, :], fb32[:, :], W_SCALE, fbh[:, :], ALU.mult,
                                           ALU.subtract).then_inc(sem("fw_ready"), 1)
            dve.wait_ge(sem("a_e_mm"), 1)
            link(nc.vector.reduce_max(a_s[:, 0, :], ps[:, 4, 0:H * TT].rearrange("p (t c) -> p t c", t=TT), AX.X))
            nc.vector.tensor_scalar(a_s[:, 1, :], a_s[:, 0, :], -(DH ** -0.5), None, ALU.mult)\
              .then_inc(sem("a_max"), 1)
            dve.wait_ge(sem("a_exp"), 1)
            link(nc.vector.reciprocal(a_s[:, 3, :], a_s[:, 2, :]))
            link(nc.vector.tensor_tensor(a_p[:, :, :], a_e[:, :, :],
                                         a_s[:, 3, :].unsqueeze(2).broadcast_to([P, TT, H]), ALU.mult))
            for n in range(2):
                ins = nc.vector.tensor_tensor(
                    a_mT[:, :, NQ * n:NQ * n + NQ].rearrange("p t (h q) -> p t h q", q=4),
                    a_p[:, :, :].unsqueeze(3).broadcast_to([P, TT, H, 4]),
                    small[:, SM_MIX + 4 * n:SM_MIX + 4 * n + 4].unsqueeze(1).unsqueeze(1)
                    .broadcast_to([P, TT, H, 4]), ALU.mult)
            ins.then_inc(sem("a_mT"), 1)
            dve.wait_ge(sem("a_z_mm"), 1)
            nc.vector.tensor_copy(a_z[:, :, :], ps[:, 0:2, :].rearrange("p b (t c) -> p (b t) c", t=2))\
              .then_inc(sem("a_z"), 1)
            dve.wait_ge(sem("a_x_mm"), 1)
            o = ps[:, 2:4, :].rearrange("p b (t c) -> p (b t) c", t=2)
            link(nc.vector.tensor_tensor(x[:, :, :], x[:, :, :], o, ALU.add))
            link(nc.vector.tensor_tensor(x[:, :, :], x[:, :, :], rows[:, 0:1, :].broadcast_to([P, TT, D]), ALU.add))
            nc.vector.nop().then_inc(sem("x_attn"), 1)

            norm_x("mid")
            f = lnb["mid"]
            dve.wait_ge(sem("xh_ready"), 1)
            nc.vector.tensor_tensor(f["l"][:, :, :], f["xnT"][:, :, :], f["h"][:, :, :], ALU.subtract)\
              .then_inc(sem("xl_ready"), 1)
            dve.wait_ge(sem("f_l_mm"), 1)
            o = ps[:, 0:2, :].rearrange("p b (t c) -> p (b t) c", t=2)
            link(nc.vector.tensor_tensor(lg[:, :, :], o, rows[:, 1:2, :].broadcast_to([P, TT, D]), ALU.add))
            link(nc.vector.reduce_max(f_s[:, 2, :], lg[:, :, :], AX.X))
            nc.vector.tensor_scalar(f_s[:, 0, :], f_s[:, 2, :], -1.0, None, ALU.mult).then_inc(sem("f_m"), 1)
            dve.wait_ge(sem("f_e"), 1)
            link(nc.vector.reciprocal(f_s[:, 2, :], f_s[:, 1, :]))
            for t in range(TT):
                ins = nc.vector.max(f_t[:, t, :], ex[:, t, :])
            link(ins)
            for t in range(TT):
                ins = nc.vector.max_index(f_i[:, t, :], f_t[:, t, :], ex[:, t, :])
            link(ins)
            link(nc.vector.tensor_scalar(f_m[:, :, :], f_i[:, :, 0:1], E - 1, None, ALU.bitwise_and))
            link(nc.vector.tensor_copy(f_f[:, :].unsqueeze(2), f_m[:, :, :]))
            link(nc.vector.tensor_scalar(f_s[:, 1, :], f_s[:, 2, :], 1 / W_SCALE, None, ALU.mult))
            link(nc.vector.tensor_tensor(f_s[:, 2, :], f_s[:, 1, :], f_t[:, :, 0], ALU.mult))
            for t in range(TT):
                ins = nc.vector.tensor_scalar(f_w[:, t, :], small[:, SM_IOTA:SM_IOTA + E], f_f[:, t:t + 1],
                                              f_s[:, 2, t:t + 1], ALU.is_equal, ALU.mult)
            ins.then_inc(sem("f_w"), 1)
            for q in range(TT * E):
                t = q // E
                dve.wait_ge(sem("f_r"), q + 1)
                need(dve, "f_add", q)
                nc.vector.tensor_tensor(x[:, t, :], x[:, t, :], f_y[:, q % 4, :], ALU.add).then_inc(sem("f_add"), 1)
            dve.wait_ge(sem("f_add"), TT * E)
            split_kv(1)
            nc.vector.nop().then_inc(sem("mid_done"), 1)
            norm_x("mid")
            dve.wait_ge(sem("xn_ready"), 4 * TT)
            nc.vector.nop().then_inc(sem("mid_done"), 1)

            cross(1)

            dve.wait_ge(sem("plo_done"), 2 * KT * B)
            norm_x("ssm")
            for k in range(6):
                back = 1 << k
                dve.wait_ge(sem("scan_mm"), k + 1)
                nc.vector.tensor_tensor(st_s[:, :, back:NQ], st_s[:, :, back:NQ],
                                        ps[0:N, 3, 0:B * (NQ - back)].rearrange("n (b q) -> n b q", b=B),
                                        ALU.add).then_inc(sem("scan"), 1)
            link(nc.vector.memset(g_z[:, :, :], 0.0))
            dve.wait_ge(sem("gelu"), 1)
            for ins in layernorm("ssm", g_a, g_n):
                pass
            link(ins)
            link(nc.vector.tensor_tensor(g_a[:, :, :], g_n[:, :, :], rows[:, 3:4, :].broadcast_to([P, TT, D]), ALU.mult))
            link(nc.vector.tensor_tensor(g_n[:, :, :], g_a[:, :, :], rows[:, 4:5, :].broadcast_to([P, TT, D]), ALU.add))
            link(nc.vector.tensor_scalar(g_f[:, :, :], g_n[:, :, :], 0.0, 0.0, ALU.mult, ALU.is_equal))
            link(nc.vector.copy_predicated(g_z[:, :, :], g_f[:, :, :], g_n[:, :, :]))
            link(nc.vector.tensor_scalar(g_m[:, :, :], g_n[:, :, :], F32_MAX, CLAMP, ALU.is_gt, ALU.mult))
            link(nc.vector.tensor_tensor(g_z[:, :, :], g_z[:, :, :], g_m[:, :, :], ALU.add))
            link(nc.vector.tensor_scalar(g_m[:, :, :], g_n[:, :, :], -F32_MAX, -CLAMP, ALU.is_lt, ALU.mult))
            link(nc.vector.tensor_tensor(g_z[:, :, :], g_z[:, :, :], g_m[:, :, :], ALU.add))
            link(nc.vector.tensor_tensor(x[:, :, :], x[:, :, :], g_z[:, :, :], ALU.add))
            nc.vector.nop().then_inc(sem("moe_free"), 2)

            for h in range(2):
                dve.wait_ge(sem(f"parts_in{h}"), 32 * B)
            dve.wait_ge(sem("moe_free"), 3)
            norm_x("moe")
            xn = lnb["moe"]["xn"]

            def split_w(w):
                dve.wait_ge(sem("whi_done"), w + 1)
                nc.vector.scalar_tensor_tensor(wl[:, w % 2, :], w32[:, w % 3, :], W_SCALE, wh[:, w % 2, :],
                                               ALU.mult, ALU.subtract).then_inc(sem("wlo_done"), 1)

            def top2(lo, hi, n):
                for i in range(lo, hi):
                    ins = nc.vector.max(top[:, i, :], lgm[:, i, :])
                link(ins)
                for i in range(lo, hi):
                    ins = nc.vector.max_index(topi[:, i, :], top[:, i, :], lgm[:, i, :])
                link(ins)
                nc.vector.tensor_copy(topf[:, lo:hi, :], topi[:, lo:hi, 0:2])
                nc.vector.tensor_tensor(prt[:, lo:hi, 1:2], top[:, lo:hi, 1:2], top[:, lo:hi, 0:1], ALU.subtract)\
                  .then_inc(sem("r_top"), 1)
                dve.wait_ge(sem("r_exp"), n + 1)
                link(nc.vector.tensor_scalar(prt[:, lo:hi, 0:1], pr[:, lo:hi, 1:2], 1.0, None, ALU.add))
                link(nc.vector.reciprocal(pr[:, lo:hi, 0:1], prt[:, lo:hi, 0:1]))
                link(nc.vector.tensor_tensor(prt[:, lo:hi, 1:2], pr[:, lo:hi, 1:2], pr[:, lo:hi, 0:1], ALU.mult))
                for i in range(lo, hi):
                    nc.vector.tensor_scalar(cmb[:, i, :], small[:, SM_IOTA:SM_IOTA + E], topf[:, i, 0:1],
                                            pr[:, i, 0:1], ALU.is_equal, ALU.mult)
                    ins = nc.vector.tensor_scalar(cmb2[:, i, :], small[:, SM_IOTA:SM_IOTA + E], topf[:, i, 1:2],
                                                  prt[:, i, 1:2], ALU.is_equal, ALU.mult)
                link(ins)
                link(nc.vector.tensor_tensor(cmb[:, lo:hi, :], cmb[:, lo:hi, :], cmb2[:, lo:hi, :], ALU.add))

            split_w(0)
            dve.wait_ge(sem("r_mm"), 1)
            link(nc.vector.tensor_copy(
                lgm[:, 0:2 * TT, :].rearrange("p (r t) e -> p r t e", r=2),
                ps[:, 6, 0:2 * E * TT].rearrange("p (t r e) -> p r t e", r=2, e=E)))
            top2(0, 2 * TT, 0)

            def scale_tokens(i):
                r, e = i // E, i % E
                if i >= 2:
                    dve.wait_ge(sem("xcT_mm"), i - 1)
                for t in range(TT):
                    ins = nc.vector.tensor_scalar(xc[:, i % 2, t, :], xn[:, t, :], cmb[:, TT * r + t, e:e + 1], None,
                                                  ALU.mult)
                ins.then_inc(sem("xc_ready0"), 1)

            nc.vector.nop().then_inc(sem("cmb_ready"), 1)
            scale_tokens(0)
            for i in range(2 * E):
                dve.wait_ge(sem("xch_ready"), i + 1)
                b_ = 4 + 2 * (i % 2)
                nc.vector.tensor_tensor(xcl[i // E][:, i % E, :, :], ps[:, b_:b_ + 2, :], xch[i // E][:, i % E, :, :],
                                        ALU.subtract).then_inc(sem("xcl_ready"), 1)
                if i % 2 == 0 and i + 2 < 2 * E:
                    scale_tokens(i + 2)
                if i in (E // 2, E):
                    split_w(i // (E // 2))
            for it in range(IT):
                if it < IT - 1:
                    split_w(2 * it + 3)
                g_ps, u_ps = ps[:, 2 * (it % 2), :], ps[:, 2 * (it % 2) + 1, :]
                dve.wait_ge(sem("sg"), it + 1)
                link(nc.vector.tensor_scalar(sg[:, 1, :], sg[:, 0, :], 1.0, None, ALU.add))
                link(nc.vector.reciprocal(sg[:, 2, :], sg[:, 1, :]))
                link(nc.vector.tensor_tensor(sg[:, 1, :], sg[:, 2, :], g_ps, ALU.mult))
                dve.wait_ge(sem("gu_mm"), 2 * it + 2)
                if it >= 2:
                    dve.wait_ge(sem("ilo_done"), it - 1)
                    dve.wait_ge(sem("rd_mm"), it - 1)
                nc.vector.scalar_tensor_tensor(i32[:, it % 2, :], u_ps, 1 / (W_SCALE * W_SCALE), sg[:, 1, :],
                                               ALU.mult, ALU.mult).then_inc(sem("inter"), 1)
                if it < IT - 1:
                    split_w(2 * it + 4)
            split_w(2 * IT + 1)
            dve.wait_ge(sem("ld_mm"), 1)
            link(nc.vector.tensor_copy(lgm[:, 2 * TT:3 * TT, :],
                                       ps[:, 5, 0:E * TT].rearrange("p (t e) -> p t e", t=TT)))
            top2(2 * TT, 3 * TT, 1)
            link(nc.vector.tensor_scalar(cmb2[:, 2 * TT:3 * TT, :], cmb[:, 2 * TT:3 * TT, :], 1 / W_SCALE, None,
                                         ALU.mult))
            for e in range(E):
                dve.wait_ge(sem("d_mm"), e + 1)
                if e + 2 < E:
                    split_w(2 * IT + e + 2)
                need(dve, "y_added", e)
                for t in range(TT):
                    o = ps[:, 2 * (e % 2) + t // 2, D * (t % 2):D * (t % 2) + D]
                    ins = nc.vector.scalar_tensor_tensor(x[:, t, :], o, cmb2[:, 2 * TT + t, e:e + 1], x[:, t, :],
                                                         ALU.mult, ALU.add)
                ins.then_inc(sem("y_added"), 1)
            dve.wait_ge(sem("y_added"), E)
            nc.vector.nop().then_inc(sem("x_final"), 1)


def lay_out(a):
    def chunks(w):
        return w.reshape(-1, P, w.shape[1]).transpose(1, 0, 2)

    d = {}
    d["x"] = a["x"].reshape(TT, P, D).transpose(1, 0, 2)
    d["ctxT"] = a["ctx_1024"].transpose(0, 2, 1).reshape(B, KC, P, S).transpose(0, 2, 1, 3)
    d["wkv"] = np.stack([np.stack([chunks(a[f"L{i}_xattn_Wk"].T), chunks(a[f"L{i}_xattn_Wv"].T)], 2) for i in range(2)])
    d["wq"] = np.stack([chunks(a[f"L{i}_xattn_Wq"].T) for i in range(2)])
    d["wo"] = np.stack([a[f"L{i}_xattn_Wo"].T.reshape(NP, 2, DH, D).transpose(0, 2, 1, 3).reshape(P, 2, D)
                        for i in range(2)])
    d["aw"] = np.stack([chunks(a[f"L0_attn_W{n}"]) for n in "qkvo"], 1)
    d["bias"] = np.stack([a["L1_xattn_bq"].reshape(2, P).T, a["L1_xattn_bk"].reshape(2, P).T,
                          a["L1_xattn_bv"].reshape(NP, 2, DH).transpose(0, 2, 1).reshape(P, 2)], 1)
    rows = np.stack([a["L0_attn_bo"], a["L0_ffn_bg"], a["L1_xattn_bo"], a["L1_attn_gamma"], a["L1_attn_beta"]])
    d["rows"] = np.broadcast_to(rows, (P, 5, D))
    d["fw"] = a["L0_ffn_We"].transpose(1, 0, 2).reshape(KC, P, E * D).transpose(1, 0, 2)
    d["fb"] = a["L0_ffn_be"].reshape(1, E * D)
    d["wg"] = chunks(a["L0_ffn_Wg"])
    d["am"] = np.stack([a["L1_attn_A"], a["L1_attn_A"].T], 1)
    d["bT"] = chunks(a["L1_attn_B"].T)
    d["cT"] = a["L1_attn_C"].T
    d["rw"] = np.stack([chunks(a["L1_ffn_router_gate"].T), chunks(a["L1_ffn_router_up"].T)], 2)
    d["rdw"] = chunks(a["L1_ffn_router_down"].T)
    gu = np.stack([a["L1_ffn_w_gate"], a["L1_ffn_w_up"]])
    d["wgu"] = gu.reshape(2, E, IT, P, KC, P).transpose(2, 0, 5, 4, 1, 3).reshape(2 * IT, P, KC * E * P)
    d["wd"] = a["L1_ffn_w_down"].reshape(E, D, IT, P).transpose(0, 3, 2, 1).reshape(E, P, IT * D)
    d["ident"] = np.eye(P, dtype=np.float32)
    small = np.zeros((P, 24), np.float32)
    small[:, 0] = np.arange(P) % 32 < DH
    small[:, 1] = np.arange(P) % 32 >= DH
    small[:, 2:2 + E] = np.arange(E)
    for n in range(2):
        for q in range(4):
            small[:, 10 + 4 * n + q] = (np.arange(P) // NQ == n) & (np.arange(P) % 4 == q)
    d["small"] = small
    d["ones"] = np.full((1, NP, S), M_SCALE, np.float16)
    return {k: np.ascontiguousarray(w) for k, w in d.items()}


def kernel(**inputs):
    import concourse.bacc as bacc
    from concourse.bass_utils import run_bass_kernel_spmd

    arrays = lay_out({k: np.asarray(w) for k, w in inputs.items()})
    nc = bacc.Bacc("TRN2", target_bir_lowering=False, num_devices=1)
    d = {k: nc.dram_tensor(f"in_{k}", w.shape, mybir.dt.from_np(w.dtype), kind="ExternalInput").ap()
         for k, w in arrays.items()}
    d["scratch"] = nc.dram_tensor("scratch", (B, H, NQ, DH), F32, kind="Internal").ap()
    d["cparts"] = nc.dram_tensor("cparts", (B, 2, P, KC, S), mybir.dt.float16, kind="Internal").ap()
    d["qscratch"] = nc.dram_tensor("qscratch", (2, P, 2, 2 * T), mybir.dt.float16, kind="Internal").ap()
    out = nc.dram_tensor("out", (T, D), F32, kind="ExternalOutput").ap()
    build(nc, d, out.rearrange("(t p) c -> p t c", p=P))
    r = run_bass_kernel_spmd(nc, [{f"in_{k}": w for k, w in arrays.items()}], core_ids=[0])
    return r.results[0]["out"].reshape(B, NQ, D)
```
